# Optimizing a Trainium2 kernel written in Bass

```python
import numpy as np
import jax
import jax.numpy as jnp

def _softmax(x, axis=-1):
    return jax.nn.softmax(x, axis=axis)

def _gelu(x):
    return jax.nn.gelu(x, approximate=True)

def _silu(x):
    return jax.nn.silu(x)

def _sigmoid(x):
    return jax.nn.sigmoid(x)

def _layernorm(x, axis=-1, eps=1e-05):
    m = jnp.mean(x, axis=axis, keepdims=True)
    v = jnp.var(x, axis=axis, keepdims=True)
    return (x - m) / jnp.sqrt(v + eps)

def _scatter_add(tgt, idx, src, axis=0):
    return tgt.at[idx].add(src)

def _segment_sum(src, seg, n):
    return jax.ops.segment_sum(src, seg, n)
kernel_name = 'mk_adj_preln_d2_adj_r2_82af00'

def setup_inputs(seed: int=0):
    np.random.seed(seed)
    _w = jnp.asarray

    def _rec_inputs():
        import jax
        import jax.numpy as jnp
        _gk = jax.random.key(seed)
        x = -9.806e-05 + 1 * jax.random.normal(jax.random.fold_in(_gk, 1), (4096, 64), jnp.float32)
        _w = (1.0 + jnp.arange(4096, dtype=jnp.float32)) ** (-0.5)
        _w = _w / _w.mean()
        _pij = jnp.clip(0.00195312 * _w[:, None] * _w[None, :], 0.0, 1.0)
        _a = jax.random.uniform(jax.random.fold_in(_gk, 2), (4096, 4096)) < _pij
        adj = _a.astype(jnp.int32)
        return (x, adj)
    x, adj = _rec_inputs()

    def _L0_gnn_setup():
        import jax, jax.numpy as jnp
        import numpy as np
        ALPHA = 0.2
        NEG_BIG = jnp.float32(-9000000000000000.0)
        key = jax.random.key(seed)
        k1, k2, k3, k4 = jax.random.split(key, 4)
        N, F_IN, F_OUT = (4096, 64, 64)
        inputs = jax.random.normal(k1, (N, F_IN), dtype=jnp.float32)
        adj = jax.random.randint(k2, (N, N), 0, 2, dtype=jnp.int32)
        gain = 1.414
        lim_w = gain * np.sqrt(6.0 / (F_IN + F_OUT))
        W = jax.random.uniform(k3, (F_IN, F_OUT), dtype=jnp.float32, minval=-lim_w, maxval=lim_w)
        lim_a = gain * np.sqrt(6.0 / (2 * F_OUT + 1))
        a = jax.random.uniform(k4, (2 * F_OUT, 1), dtype=jnp.float32, minval=-lim_a, maxval=lim_a)
        return {'inputs': inputs, 'adj': adj, 'W': W, 'a': a}
    _L0_gnn_all = _L0_gnn_setup()
    _L0_gnn_in = {k: v for k, v in _L0_gnn_all.items() if k in ('W', 'a')}
    del _L0_gnn_all

    def _L1_gnn_setup():
        import jax, jax.numpy as jnp
        import numpy as np
        N = 1024
        ATOM_D = 64
        H = 8
        NB = 8
        D = ATOM_D * H
        NEG_SLOPE = 0.2
        key = jax.random.key(seed)
        ks = jax.random.split(key, 12)
        inp = {'atom_embeddings': jax.random.normal(ks[0], (N, ATOM_D), dtype=jnp.float32), 'edges': jax.random.randint(ks[1], (N, N), -1, NB, dtype=jnp.int32), 'Qw': jax.random.normal(ks[2], (ATOM_D, D), dtype=jnp.float32) / np.sqrt(ATOM_D), 'Qb': jnp.zeros((D,), dtype=jnp.float32), 'Kw': jax.random.normal(ks[3], (ATOM_D, D), dtype=jnp.float32) / np.sqrt(ATOM_D), 'Kb': jnp.zeros((D,), dtype=jnp.float32), 'Vw': jax.random.normal(ks[4], (ATOM_D, D), dtype=jnp.float32) / np.sqrt(ATOM_D), 'Vb': jnp.zeros((D,), dtype=jnp.float32), 'a': jax.random.normal(ks[5], (NB, 2 * D, H), dtype=jnp.float32) * np.sqrt(2.0 / (2 * D + H)) * 1.414, 'Pw': jax.random.normal(ks[6], (D, ATOM_D), dtype=jnp.float32) / np.sqrt(D), 'Pb': jnp.zeros((ATOM_D,), dtype=jnp.float32)}
        return inp
    _L1_gnn_all = _L1_gnn_setup()
    _L1_gnn_in = {k: v for k, v in _L1_gnn_all.items() if k in ('Qw', 'Qb', 'Kw', 'Kb', 'Vw', 'Vb', 'a', 'Pw', 'Pb')}
    del _L1_gnn_all
    return {'x': x, 'adj': adj, 'L0_gnn_W': _L0_gnn_in['W'], 'L0_gnn_a': _L0_gnn_in['a'], 'L1_gnn_Qw': _L1_gnn_in['Qw'], 'L1_gnn_Qb': _L1_gnn_in['Qb'], 'L1_gnn_Kw': _L1_gnn_in['Kw'], 'L1_gnn_Kb': _L1_gnn_in['Kb'], 'L1_gnn_Vw': _L1_gnn_in['Vw'], 'L1_gnn_Vb': _L1_gnn_in['Vb'], 'L1_gnn_a': _L1_gnn_in['a'], 'L1_gnn_Pw': _L1_gnn_in['Pw'], 'L1_gnn_Pb': _L1_gnn_in['Pb']}

def reference(x, adj, L0_gnn_W, L0_gnn_a, L1_gnn_Qw, L1_gnn_Qb, L1_gnn_Kw, L1_gnn_Kb, L1_gnn_Vw, L1_gnn_Vb, L1_gnn_a, L1_gnn_Pw, L1_gnn_Pb):
    import jax
    import jax.numpy as jnp

    def _L0_gnn_ref(inputs, adj, W, a):
        import jax, jax.numpy as jnp
        import numpy as np
        ALPHA = 0.2
        NEG_BIG = jnp.float32(-9000000000000000.0)
        Wh = inputs @ W
        F_out = W.shape[1]
        a_src = a[:F_out, 0]
        a_dst = a[F_out:, 0]
        e = (Wh @ a_src)[:, None] + (Wh @ a_dst)[None, :]
        e = jnp.where(e > 0, e, ALPHA * e)
        scores = jnp.where(adj > 0, e, NEG_BIG)
        attention = jax.nn.softmax(scores, axis=1)
        h_prime = attention @ Wh
        return jax.nn.elu(h_prime)

    def _L1_gnn_ref(atom_embeddings, edges, Qw, Qb, Kw, Kb, Vw, Vb, a, Pw, Pb):
        import jax, jax.numpy as jnp
        import numpy as np
        N = 1024
        ATOM_D = 64
        H = 8
        NB = 8
        D = ATOM_D * H
        NEG_SLOPE = 0.2
        n, d = atom_embeddings.shape
        nb, two_d, h = a.shape
        D_ = two_d // 2
        Q = atom_embeddings @ Qw + Qb
        K = atom_embeddings @ Kw + Kb
        V = atom_embeddings @ Vw + Vb
        A1 = a[:, :D_, :]
        A2 = a[:, D_:, :]
        S1 = jnp.einsum('id,kdh->ikh', Q, A1)
        S2 = jnp.einsum('jd,kdh->jkh', K, A2)
        kidx = jnp.clip(edges, 0, nb - 1)
        rows = jnp.arange(n)
        e = S1[rows[:, None], kidx] + S2[rows[None, :], kidx]
        valid = (edges >= 0)[..., None]
        e = jnp.where(valid, jax.nn.leaky_relu(e, negative_slope=NEG_SLOPE), 0.0)
        attn = jax.nn.softmax(e, axis=1)
        Vh = V.reshape(n, h, d)
        out = jnp.einsum('ijh,jhd->ihd', attn, Vh).reshape(n, h * d)
        return out @ Pw + Pb
    h = jnp.maximum(_layernorm(x, axis=-1), 0.0)
    x = x + _L0_gnn_ref(h, adj, L0_gnn_W, L0_gnn_a)
    h = jnp.maximum(_layernorm(x, axis=-1), 0.0)
    x = x + _L1_gnn_ref(h, adj, L1_gnn_Qw, L1_gnn_Qb, L1_gnn_Kw, L1_gnn_Kb, L1_gnn_Vw, L1_gnn_Vb, L1_gnn_a, L1_gnn_Pw, L1_gnn_Pb)
    return x

_drawn_inputs = setup_inputs


def setup_inputs(seed=0):
    import zlib

    import numpy as np

    out = dict(_drawn_inputs(seed))
    spreads = {'L1_gnn_Qb': (0.0, 2.0),
     'L1_gnn_Kb': (0.0, 2.0),
     'L1_gnn_Vb': (0.0, 0.1),
     'L1_gnn_Pb': (0.0, 0.1)}
    factors = {'L1_gnn_Qw': 3.672}
    for name, (base, spread) in spreads.items():
        noise = np.random.default_rng([zlib.crc32(name.encode()), seed]).standard_normal(out[name].shape)
        drawn = base * np.exp(spread * noise) if base else spread * noise
        out[name] = jnp.asarray(drawn.astype(out[name].dtype))
    for name, factor in factors.items():
        out[name] = (out[name] * factor).astype(out[name].dtype)
    return out
```

```python
from contextlib import ExitStack

import concourse.bass as bass
from concourse import mybir


def two_layer_graph_attention(nc, x, adj, W0, a0, Qw, Qb, Kw, Kb, Vw, Vb, a1, Pw, Pb, out):
    f32 = mybir.dt.float32
    bf16 = mybir.dt.bfloat16
    i8 = mybir.dt.int8
    i32 = mybir.dt.int32
    ALU = mybir.AluOpType
    ACT = mybir.ActivationFunctionType
    AX = mybir.AxisListType

    N, F = x.shape
    P = 128
    NT = N // P
    CH = 512
    NI = N // CH
    IB = CH // P
    KC, _, H = a1.shape
    HD = H * F
    CL = KC + 1
    KH = CL * H
    KHV = KC * H
    DC = HD // P
    NQ = H // 4
    G8 = 8
    NG = NT // G8
    SLOPE = 0.2
    EPS = 1e-5
    ABSENT = 1e30

    x_v = x.rearrange("(t p) f -> p t f", p=P)
    out_v = out.rearrange("(t p) f -> p t f", p=P)
    adj_v = adj.rearrange("(m p) j -> m p j", p=P)
    code_dram = nc.dram_tensor("code_scratch", (NI * P, NT * CH), i8).ap()
    r_dram = nc.dram_tensor("r_scratch", (KH, N), f32).ap()

    ctx = ExitStack()
    with ctx:
        def sem(name):
            return ctx.enter_context(nc.semaphore(name))

        def sb(scope, name, shape, dt):
            return scope.enter_context(nc.sbuf_tensor(name, shape, dt))

        xs = sb(ctx, "xs", [P, NT, F], f32)
        identF = sb(ctx, "identF", [P, P], f32)
        identB = sb(ctx, "identB", [P, P], bf16)
        onesB = sb(ctx, "onesB", [P, 1], bf16)
        onesF = sb(ctx, "onesF", [P, 1], f32)
        stat = sb(ctx, "stat", [P, 5, NT], f32)
        pb = sb(ctx, "pb", [P, F], f32)
        classneg = sb(ctx, "classneg", [P, CL], f32)
        flagcol = sb(ctx, "flagcol", [P, 4], f32)
        flagi = sb(ctx, "flagi", [P, 1], i32)

        wsc = ExitStack()
        qw = sb(wsc, "qw", [F + 1, HD], f32)
        kw = sb(wsc, "kw", [F + 1, HD], f32)
        vw = sb(wsc, "vw", [F + 1, HD], f32)
        av = sb(wsc, "av", [P, 2 * DC, KC, H], f32)
        pw = sb(wsc, "pw", [F, H, F], f32)
        meanmat = sb(wsc, "meanmat", [P, P], f32)
        zerosB = sb(wsc, "zerosB", [P, P + 1], bf16)
        flagscr = sb(wsc, "flagscr", [P, P], f32)
        h0 = sb(wsc, "h0", [P, NT, F], f32)

        l0 = ExitStack()
        raw = sb(l0, "raw", [P, 2, N], i32)
        abf = sb(l0, "abf", [P, 2, N], bf16)
        code0 = sb(l0, "code0", [P, NT, CH], i8)
        pos0 = sb(l0, "pos0", [P, NT, CH], i8)
        r0 = sb(l0, "r0", [P, N], f32)
        T0 = sb(l0, "T0", [P, 4, CH], f32)
        sq0 = sb(l0, "sq0", [P, NT, F], f32)
        h0T = raw[0:F, 1, :].bitcast(f32)
        wh = sb(l0, "wh", [P, NT, F + 2], f32)
        w0s = sb(l0, "w0s", [F, F + 2], f32)
        w0T = sb(l0, "w0T", [F, F], f32)
        a0s = sb(l0, "a0s", [F, 2], f32)
        wrep = sb(l0, "wrep", [F, P], f32)
        W0e = sb(l0, "W0e", [P, NT, F + 1], f32)
        th0 = sb(l0, "th0", [P, NT], f32)
        d0 = sb(l0, "d0", [P, NT], f32)
        dm = sb(l0, "dm", [P, 4], f32)
        whsum = sb(l0, "whsum", [P, F], f32)
        whmean = sb(l0, "whmean", [P, F], f32)
        A0s = sb(l0, "A0s", [F + 1, CH], f32)
        fin0 = sb(l0, "fin0", [P, 4, IB, F], f32)
        den0 = sb(l0, "den0", [P, 4, IB], f32)
        l0.close()
        wsc.close()

        l1 = ExitStack()
        vp = sb(l1, "vp", [P, NT, HD], f32)
        th = sb(l1, "th", [P, NT, KH], f32)
        dd = sb(l1, "dd", [P, NT, KH], f32)
        LL = sb(l1, "LL", [P, NT, KH], f32)
        code = sb(l1, "code", [P, NT, CH], i8)
        pre = ExitStack()
        hT = sb(pre, "hT", [F + 1, N], f32)
        rT = sb(pre, "rT", [KH, N], f32)
        h1 = sb(pre, "h1", [P, NT, F], f32)
        sq1 = sb(pre, "sq1", [P, NT, F], f32)
        bt = sb(pre, "bt", [P, NT, KH], f32)
        qT = sb(pre, "qT", [P, DC, F + 1], f32)
        kT = sb(pre, "kT", [P, DC, F + 1], f32)
        vT = sb(pre, "vT", [F, H, F + 1], f32)
        sa = sb(pre, "sa", [F + 1, KH], f32)
        sbm = sb(pre, "sbm", [F + 1, KH], f32)
        vpw = sb(pre, "vpw", [F + 1, HD], f32)
        bm8 = sb(pre, "bm8", [KH, NI + 1], f32)
        bmrep = sb(pre, "bmrep", [KH, P], f32)
        bmx = sb(pre, "bmx", [P, KH], f32)
        pre.close()
        R = sb(l1, "R", [P, 2, H, CH], f32)
        T = sb(l1, "T", [P, H, CH], f32)
        Ws = sb(l1, "Ws", [P, 2, H, F], f32)
        Ds = sb(l1, "Ds", [P, 2, H, 32], f32)
        Mt = sb(l1, "Mt", [P, 2, CH], bf16)
        M = sb(l1, "M", [P, 2, CH], bf16)
        accS = sb(l1, "accS", [P, 6, CH], f32)
        accT = sb(l1, "accT", [P, IB, H, F], f32)
        O = sb(l1, "O", [P, IB, H, F], f32)
        tmp = sb(l1, "tmp", [P, H, F], f32)
        denT = sb(l1, "denT", [P, IB, H], f32)
        tiny = sb(l1, "tiny", [P, 4, IB * H], f32)
        abarg = sb(l1, "abarg", [P, 2, IB * H], f32)
        ab = sb(l1, "ab", [P, 2, IB * H], f32)
        cst = sb(l1, "cst", [P, IB * H], f32)
        den = sb(l1, "den", [P, IB * H], f32)
        rden = sb(l1, "rden", [P, IB * H], f32)
        res = sb(l1, "res", [P, IB, F], f32)
        l1.close()

        ps = ctx.enter_context(nc.psum_tensor("ps", [P, 8, CH], f32))

        ld_x, ld_w0, ld_l1 = sem("ld_x"), sem("ld_w0"), sem("ld_l1")
        consts = sem("consts")
        vstep, astep, pstep = sem("vstep"), sem("astep"), sem("pstep")
        ln_var, ln_std, ln_done = sem("ln_var"), sem("ln_std"), sem("ln_done")
        hT_ps, hT_sb = sem("hT_ps"), sem("hT_sb")
        w0T_ps, w0T_sb, wa_ps, wa_sb = sem("w0T_ps"), sem("w0T_sb"), sem("wa_ps"), sem("wa_sb")
        wh_ps, wh_sb = sem("wh_ps"), sem("wh_sb")
        dmax_in, dmax_out, dshift, dexp = sem("dmax_in"), sem("dmax_out"), sem("dshift"), sem("dexp")
        rrow_ps, rrow_z, rrow_done = sem("rrow_ps"), sem("rrow_z"), sem("rrow_done")
        w0_ready, mean_in, mean_ps, mean_sb = sem("w0_ready"), sem("mean_in"), sem("mean_ps"), sem("mean_sb")
        raw_ld = [sem("raw_ld0"), sem("raw_ld1")]
        cast_done, blk_done, tg_done, ev_done = sem("cast_done"), sem("blk_done"), sem("tg_done"), sem("ev_done")
        pos_done, code_st = sem("pos_done"), sem("code_st")
        t0_made, t0_used = sem("t0_made"), sem("t0_used")
        a0_sb, a0_tr, a0_fin = sem("a0_sb"), sem("a0_tr"), sem("a0_fin")
        flag_ps, flag_sum, flag_tot, flag_done = sem("flag_ps"), sem("flag_sum"), sem("flag_tot"), sem("flag_done")
        elu_in, elu_exp = sem("elu_in"), sem("elu_exp")
        l0_end = sem("l0_end")
        wT_ps, wT_sb, s_ps, s_sb = sem("wT_ps"), sem("wT_sb"), sem("s_ps"), sem("s_sb")
        bT_ps, bT_red, bmx_in, bmx_ps, bmx_sb = sem("bT_ps"), sem("bT_red"), sem("bmx_in"), sem("bmx_ps"), sem("bmx_sb")
        ab_ps, ab_sb, aT_ps, aT_z, rT_done, rT_st = (sem("ab_ps"), sem("ab_sb"), sem("aT_ps"), sem("aT_z"),
                                                   sem("rT_done"), sem("rT_st"))
        tab_in, tab_exp, vp_ps, vp_sb = sem("tab_in"), sem("tab_exp"), sem("vp_ps"), sem("vp_sb")
        pre_end = sem("pre_end")
        r_ld = [sem("r_ld0"), sem("r_ld1")]
        code_ld = [sem("code_ld0"), sem("code_ld1")]
        abs_done, mask_made, t_made, pe_quad = sem("abs_done"), sem("mask_made"), sem("t_made"), sem("pe_quad")
        w_staged, acc_ev, acc_tr, accT_done = sem("w_staged"), sem("acc_ev"), sem("acc_tr"), sem("accT_done")
        ab_arg, ab_done, merged, den_fin, rden_ok = (sem("ab_arg"), sem("ab_done"), sem("merged"), sem("den_fin"),
                                                    sem("rden_ok"))
        mstep, fstep = sem("mstep"), sem("fstep")
        out_st = sem("out_st")
        passed = sem("passed")

        class Chain:

            def __init__(self, eng, s):
                self.eng, self.s, self.n = eng, s, 0

            def __call__(self, ins):
                self.n += 1
                ins.then_inc(self.s, 1)
                self.eng.wait_ge(self.s, self.n)

        def held(eng, s, value):
            eng.wait_ge(s, value)
            eng.sem_inc(passed, 1)

        def layernorm(dve, link, src, cen, sq, which):
            s, mean, v, rr, t = (stat[:, n, :] for n in range(5))

            def wide(a):
                return a.unsqueeze(2).to_broadcast([P, NT, F])
            link(nc.vector.tensor_reduce(s, src, AX.X, ALU.add))
            link(nc.vector.tensor_scalar(mean, s, 1.0 / F, None, ALU.mult))
            link(nc.vector.tensor_tensor(cen, src, wide(mean), ALU.subtract))
            link(nc.vector.tensor_tensor(sq, cen, cen, ALU.mult))
            link(nc.vector.tensor_reduce(s, sq, AX.X, ALU.add))
            nc.vector.tensor_scalar(v, s, 1.0 / F, EPS, ALU.mult, ALU.add).then_inc(ln_var, 1)
            dve.wait_ge(ln_var, which)
            dve.wait_ge(ln_std, which)
            link(nc.vector.reciprocal(rr, t))
            link(nc.vector.tensor_tensor(t, rr, rr, ALU.mult))
            link(nc.vector.tensor_tensor(t, t, v, ALU.mult))
            link(nc.vector.tensor_scalar(t, t, -0.5, 1.5, ALU.mult, ALU.add))
            link(nc.vector.tensor_tensor(rr, rr, t, ALU.mult))
            nc.vector.scalar_tensor_tensor(out=cen, in0=cen, scalar=0.0, in1=wide(rr), op0=ALU.max,
                                           op1=ALU.mult).then_inc(ln_done, 1)
            dve.wait_ge(ln_done, which)

        def class_steps(eng, kvals, step, tail):
            n = len(kvals)
            u = 1 if n % 2 == 0 else 2

            def body(I, peeled):
                for e in range(u):
                    for c in range(n):
                        s = e * n + c
                        step(I * (u * n) + s, I * (u * n // 2) + s // 2, I * u + e, c, peeled and s == 0,
                             s % 2, peeled and s < 2)
            body(0, True)
            with eng.Fori(1, NI // u) as I:
                body(I, False)
            tail(NI * n, NI - 1)

        def both_paths(eng, engine_type, program):
            eng.wait_ge(flag_done, 1)
            flag = eng.value_load(flagi[0:1, 0:1], min_val=0, max_val=1)
            with eng.If(flag < 1):
                program([0, 1])
            with eng.Else():
                program(list(range(KC)) + [-1])

        block = ctx.enter_context(nc.Block())

        @block.sync
        def _(sp):
            sp.dma_start(xs[:, :, :], x_v).then_inc(ld_x, 16)
            sp.dma_start(w0s[:, 0:F], W0).then_inc(ld_w0, 16)
            for half in range(2):
                sp.dma_start(a0s[:, half:half + 1], a0[half * F:(half + 1) * F, :]).then_inc(ld_w0, 16)
            sp.wait_ge(rrow_ps, NI)
            with sp.Fori(0, NI) as ic:
                for b in range(IB):
                    sp.wait_ge(cast_done, ic * IB + b)
                    sp.dma_start(raw[:, b % 2, :], adj_v[bass.ds(ic * IB + b, 1), :, :].rearrange("a p j -> p (a j)"))\
                        .then_inc(raw_ld[b % 2], 16)
            sp.wait_ge(rT_done, NI)
            sp.dma_start(r_dram, rT[:, :]).then_inc(rT_st, 16)
            sp.wait_ge(rT_st, 16)
            sp.wait_ge(pre_end, 4)
            sp.wait_ge(code_st, 16 * NI)

            def program(kvals):
                n = len(kvals)

                def step(S, half, ic, c, first, par, early):
                    if not early:
                        sp.wait_ge(t_made, (S - 1) * (NT * NQ))
                    k = c
                    sp.dma_start(R[:, par, :, :],
                                 r_dram[k * H:(k + 1) * H, bass.ds(ic * CH, CH)].partition_broadcast(P))\
                        .then_inc(r_ld[par], 16)
                    if c == 0:
                        for hf in range(2):
                            if not first:
                                held(sp, mask_made, S * NT - (1 - hf) * (NT // 2))
                            w = NT // 2
                            sp.dma_start(code[:, hf * w:(hf + 1) * w, :],
                                         code_dram[bass.ds(ic * P, P), hf * w * CH:(hf + 1) * w * CH]
                                         .rearrange("p (t i) -> p t i", t=w)).then_inc(code_ld[hf], 16)

                class_steps(sp, kvals, step, lambda S, ic: None)
            both_paths(sp, "SP", program)

        @block.gpsimd
        def _(pool):
            link = Chain(pool, pstep)
            link(nc.gpsimd.memset(identF[:, :], 0.0))
            link(nc.gpsimd.memset(identB[:, :], 0.0))
            for m in (identF, identB):
                nc.gpsimd.affine_select(out=m[:, :], in_=m[:, :], compare_op=ALU.not_equal, fill=1.0, base=0,
                                        pattern=[[-1, P]], channel_multiplier=1).then_inc(consts, 1)
            nc.gpsimd.memset(meanmat[:, :], 1.0 / N).then_inc(consts, 1)
            nc.gpsimd.memset(zerosB[:, :], 0.0).then_inc(consts, 1)
            nc.gpsimd.memset(onesB[:, :], 1.0).then_inc(consts, 1)
            nc.gpsimd.memset(onesF[:, :], 1.0).then_inc(consts, 1)
            for c in range(CL):
                nc.gpsimd.memset(classneg[:, c:c + 1], float(-c if c < KC else 1)).then_inc(consts, 1)
            pool.wait_ge(dmax_in, 1)
            nc.gpsimd.partition_all_reduce(dm[:, 1:2], dm[:, 0:1], P, bass.bass_isa.ReduceOp.max)\
                .then_inc(dmax_out, 1)
            with pool.Fori(0, NI) as ic:
                held(pool, ev_done, (ic + 1) * (IB * NG))
                pool.dma_start(code_dram[bass.ds(ic * P, P), :], code0[:, :, :].rearrange("p t i -> p (t i)"))\
                    .then_inc(code_st, 16)
            pool.wait_ge(flag_sum, 1)
            nc.gpsimd.partition_all_reduce(flagcol[:, 3:4], flagcol[:, 2:3], P, bass.bass_isa.ReduceOp.max)\
                .then_inc(flag_tot, 1)
            pool.wait_ge(pre_end, 4)
            pbase = link.n

            def program(kvals):
                n = len(kvals)

                def stage(S, c, q, u, early=False):
                    jt = q * 2 + u
                    if not early:
                        held(pool, pe_quad, (S * NT + jt - 1) * NQ)
                    dj = dd[:, bass.ds(jt, 1), c * H:(c + 1) * H].rearrange("p a h -> p (a h)")
                    nc.gpsimd.tensor_tensor(Ws[:, u, :, :],
                                            vp[:, bass.ds(jt, 1), :].rearrange("p a (h f) -> p (a h) f", h=H),
                                            dj.unsqueeze(2).to_broadcast([P, H, F]), ALU.mult).then_inc(w_staged, 1)
                    nc.gpsimd.tensor_copy(Ds[:, u, :, :], dj.unsqueeze(2).to_broadcast([P, H, 32]))\
                        .then_inc(w_staged, 1)

                PER = 3 * 2 * IB
                CSTEPS = 20

                def scales(S, ic, c):
                    held(pool, accT_done, S * 6)
                    L = LL[:, bass.ds(ic * IB, IB), c * H:(c + 1) * H]
                    dT = denT[:, :, :].rearrange("p b h -> p (b h)")
                    pres, t1, t2, Lp = (tiny[:, m, :] for m in range(4))
                    base = (S - 1) * CSTEPS

                    def wide(a):
                        return a.rearrange("p (b h) -> p b h", h=H)
                    seq = [lambda: nc.gpsimd.tensor_scalar(pres, dT, 0.0, 1.0, ALU.is_gt, ALU.mult),
                           lambda: nc.gpsimd.tensor_tensor(wide(t1), L, wide(pres), ALU.mult),
                           lambda: nc.gpsimd.tensor_scalar(t2, pres, ABSENT, -ABSENT, ALU.mult, ALU.add),
                           lambda: nc.gpsimd.tensor_tensor(Lp, t1, t2, ALU.add)]
                    if c == 0:
                        seq += [lambda: nc.gpsimd.tensor_copy(cst[:, :], Lp),
                                lambda: nc.gpsimd.tensor_copy(den[:, :], dT)]
                    else:
                        seq += [lambda: nc.gpsimd.tensor_tensor(t1, Lp, cst[:, :], ALU.subtract),
                                lambda: nc.gpsimd.tensor_scalar(t1, t1, 0.0, 1.0, ALU.is_gt, ALU.mult),
                                lambda: nc.gpsimd.tensor_scalar(t2, t1, -1.0, 1.0, ALU.mult, ALU.add),
                                lambda: nc.gpsimd.tensor_tensor(t1, t1, Lp, ALU.mult),
                                lambda: nc.gpsimd.tensor_tensor(t2, t2, cst[:, :], ALU.mult),
                                lambda: nc.gpsimd.tensor_tensor(t1, t1, t2, ALU.add),
                                lambda: nc.gpsimd.tensor_tensor(abarg[:, 0, :], cst[:, :], t1, ALU.subtract),
                                lambda: nc.gpsimd.tensor_tensor(abarg[:, 1, :], Lp, t1, ALU.subtract),
                                lambda: nc.gpsimd.tensor_copy(cst[:, :], t1)]
                    for m, f in enumerate(seq):
                        f().then_inc(mstep, 1)
                        held(pool, mstep, base + m + 1)
                    m = len(seq)
                    if c > 0:
                        pool.sem_inc(ab_arg, 1)
                        held(pool, ab_done, ic * (n - 1) + c)
                        for f in (lambda: nc.gpsimd.tensor_tensor(den[:, :], den[:, :], ab[:, 0, :], ALU.mult),
                                  lambda: nc.gpsimd.tensor_tensor(t2, dT, ab[:, 1, :], ALU.mult),
                                  lambda: nc.gpsimd.tensor_tensor(den[:, :], den[:, :], t2, ALU.add)):
                            f().then_inc(mstep, 1)
                            m += 1
                            held(pool, mstep, base + m)
                    pool.sem_inc(mstep, CSTEPS - m)
                    if c == n - 1:
                        pool.sem_inc(den_fin, 1)

                def merge(S, c, piece, count):
                    A = accT[:, :, :, :].rearrange("p b (q h) f -> p (b q) h f", q=NQ)[:, bass.ds(piece, 1), :, :]\
                        .rearrange("p a h f -> p (a h) f")
                    Oq = O[:, :, :, :].rearrange("p b (q h) f -> p (b q) h f", q=NQ)[:, bass.ds(piece, 1), :, :]\
                        .rearrange("p a h f -> p (a h) f")

                    def factor(w):
                        return ab[:, w, :].rearrange("p (a h) -> p a h", h=4)[:, bass.ds(piece, 1), :]\
                            .rearrange("p a h -> p (a h)").unsqueeze(2).to_broadcast([P, 4, F])
                    if c == 0:
                        nc.gpsimd.tensor_copy(Oq, A).then_inc(merged, 1)
                        held(pool, merged, count + 1)
                        pool.sem_inc(merged, 2)
                        return
                    tq = tmp[:, 0:4, :]
                    nc.gpsimd.tensor_tensor(tq, A, factor(1), ALU.mult).then_inc(merged, 1)
                    nc.gpsimd.tensor_tensor(Oq, Oq, factor(0), ALU.mult).then_inc(merged, 1)
                    held(pool, merged, count + 2)
                    nc.gpsimd.tensor_tensor(Oq, Oq, tq, ALU.add).then_inc(merged, 1)
                    held(pool, merged, count + 3)

                FST = 6

                def finish(ic, ib, count):
                    rb = rden[:, :].rearrange("p (b h) -> p b h", h=H)[:, bass.ds(ib, 1), :]\
                        .rearrange("p a h -> p (a h)").unsqueeze(2).to_broadcast([P, H, F])
                    Ob = O[:, bass.ds(ib, 1), :, :].rearrange("p a h f -> p (a h) f")
                    rs = res[:, bass.ds(ib, 1), :].rearrange("p a f -> p (a f)")
                    xb = xs[:, bass.ds(ic * IB + ib, 1), :].rearrange("p a f -> p (a f)")
                    t = tmp
                    seq = [lambda: nc.gpsimd.tensor_tensor(t[:, :, :], Ob, rb, ALU.mult),
                           lambda: nc.gpsimd.tensor_tensor(t[:, 0:4, :], t[:, 0:4, :], t[:, 4:8, :], ALU.add),
                           lambda: nc.gpsimd.tensor_tensor(t[:, 0:2, :], t[:, 0:2, :], t[:, 2:4, :], ALU.add),
                           lambda: nc.gpsimd.tensor_tensor(t[:, 0, :], t[:, 0, :], t[:, 1, :], ALU.add),
                           lambda: nc.gpsimd.tensor_tensor(t[:, 0, :], t[:, 0, :], pb[:, :], ALU.add),
                           lambda: nc.gpsimd.tensor_tensor(rs, t[:, 0, :], xb, ALU.add)]
                    for m, f in enumerate(seq):
                        f().then_inc(fstep, 1)
                        held(pool, fstep, count + m + 1)

                def store(ic):
                    pool.dma_start(out_v[:, bass.ds(ic * IB, IB), :], res[:, :, :]).then_inc(out_st, 16)

                def step(S, half, ic, c, first, par, early):
                    pc = (c - 1) % n
                    pic = ic if c > 0 else ic - 1
                    stage(S, c, 0, 0, first)
                    stage(S, c, 0, 1, first)
                    if not first:
                        scales(S, pic, pc)
                    with pool.Fori(1, 9) as q:
                        stage(S, c, q, 0)
                        stage(S, c, q, 1)
                        if not first:
                            merge(S, pc, q - 1, (S - 1) * PER + (q - 1) * 3)
                    if pc == n - 1 and not first:
                        held(pool, rden_ok, pic + 1)
                        held(pool, out_st, pic * 16)
                        with pool.Fori(9, 13) as q:
                            stage(S, c, q, 0)
                            stage(S, c, q, 1)
                            finish(pic, q - 9, pic * (FST * IB) + (q - 9) * FST)
                        store(pic)
                        with pool.Fori(13, NT // 2) as q:
                            stage(S, c, q, 0)
                            stage(S, c, q, 1)
                    else:
                        with pool.Fori(9, NT // 2) as q:
                            stage(S, c, q, 0)
                            stage(S, c, q, 1)

                def tail(S, ic):
                    scales(S, ic, n - 1)
                    with pool.Fori(0, 2 * IB) as q:
                        merge(S, n - 1, q, (S - 1) * PER + q * 3)
                    held(pool, rden_ok, NI)
                    held(pool, out_st, ic * 16)
                    with pool.Fori(0, IB) as q:
                        finish(ic, q, ic * (FST * IB) + q * FST)
                    store(ic)
                    pool.wait_ge(out_st, NI * 16)

                class_steps(pool, kvals, step, tail)
            both_paths(pool, "Pool", program)

        @block.scalar
        def _(act):
            link = Chain(act, astep)
            for dst, w, bvec in ((qw, Qw, Qb), (kw, Kw, Kb), (vw, Vw, Vb)):
                act.dma_start(dst[0:F, :], w).then_inc(ld_l1, 16)
                act.dma_start(dst[F:F + 1, :], bvec.unsqueeze(0)).then_inc(ld_l1, 16)
            for k in range(KC):
                act.dma_start(av[:, :, k, :], a1[k].rearrange("(c p) h -> p c h", p=P)).then_inc(ld_l1, 16)
            act.dma_start(pw[:, :, :], Pw.rearrange("(h d) f -> d h f", d=F)).then_inc(ld_l1, 16)
            act.dma_start(pb[:, :], Pb.partition_broadcast(P)).then_inc(ld_l1, 16)
            act.wait_ge(ln_var, 1)
            nc.scalar.activation(stat[:, 4, :], stat[:, 2, :], ACT.Sqrt).then_inc(ln_std, 1)
            act.wait_ge(dshift, 1)
            nc.scalar.activation(th0[:, :], d0[:, :], ACT.Exp, scale=1.0 - SLOPE).then_inc(dexp, 1)
            nc.scalar.activation(W0e[:, :, F], d0[:, :], ACT.Exp, scale=SLOPE).then_inc(dexp, 1)
            for g in range(NI):
                act.wait_ge(rrow_z, g + 1)
                nc.scalar.activation(r0[:, g * CH:(g + 1) * CH], r0[:, g * CH:(g + 1) * CH], ACT.Exp,
                                     scale=-(1.0 - SLOPE)).then_inc(rrow_done, 1)

            def cast(ic, b):
                m = ic * IB + b
                act.wait_ge(raw_ld[b % 2], (ic * (IB // 2) + b // 2 + 1) * 16)
                act.wait_ge(blk_done, m)
                nc.scalar.activation(abf[:, b % 2, :], raw[:, b % 2, :], ACT.Copy).then_inc(cast_done, 1)

            def positive(ic, b):
                act.wait_ge(ev_done, (ic * IB + b + 1) * NG)
                nc.scalar.activation(pos0[:, :, b * P:(b + 1) * P], code0[:, :, b * P:(b + 1) * P], ACT.Relu)\
                    .then_inc(pos_done, 1)

            act.sem_inc(cast_done, 1)
            with act.Fori(0, NI) as ic:
                cast(ic, 0)
                cast(ic, 1)
                act.wait_ge(t0_made, ic * NT)
                for b in range(IB):
                    positive(ic, b)
                    if b + 2 < IB:
                        cast(ic, b + 2)
            act.wait_ge(elu_in, 1)
            nc.scalar.activation(sq1[:, :, :], sq1[:, :, :], ACT.Exp).then_inc(elu_exp, 1)
            act.wait_ge(ln_var, 2)
            nc.scalar.activation(stat[:, 4, :], stat[:, 2, :], ACT.Sqrt).then_inc(ln_std, 1)
            for g in range(NI):
                act.wait_ge(aT_z, g + 1)
                nc.scalar.activation(rT[:, g * CH:(g + 1) * CH], rT[:, g * CH:(g + 1) * CH], ACT.Exp,
                                     scale=-(1.0 - SLOPE)).then_inc(rT_done, 1)
            act.wait_ge(tab_in, 1)
            nc.scalar.activation(th[:, :, :], bt[:, :, :], ACT.Exp, scale=1.0 - SLOPE).then_inc(tab_exp, 1)
            nc.scalar.activation(dd[:, :, :], bt[:, :, :], ACT.Exp, scale=SLOPE).then_inc(tab_exp, 1)
            for t in range(NT):
                act.wait_ge(vp_ps, t + 1)
                nc.scalar.activation(vp[:, t, :], ps[:, 4 + t % 4, :], ACT.Copy).then_inc(vp_sb, 1)
            act.wait_ge(vp_sb, NT)
            act.wait_ge(tab_exp, 2)
            act.sem_inc(pre_end, 1)
            act.wait_ge(pre_end, 4)

            def program(kvals):
                n = len(kvals)

                def mask(S, c, q, u, early=False):
                    jt = q * 2 + u
                    num = S * NT + jt
                    if not early:
                        act.wait_ge(mask_made, num - 1)
                        held(act, t_made, (num - 1) * NQ)
                    nc.scalar.activation(Mt[:, u, :], code[:, bass.ds(jt, 1), :].rearrange("p a i -> p (a i)"),
                                         ACT.Abs, bias=classneg[:, c:c + 1]).then_inc(abs_done, 1)
                    act.wait_ge(abs_done, num + 1)
                    nc.scalar.activation(M[:, u, :], Mt[:, u, :], ACT.Relu, bias=onesF[:, 0:1], scale=-1.0)\
                        .then_inc(mask_made, 1)

                def factors(ic, c):
                    act.wait_ge(ab_arg, ic * (n - 1) + c)
                    nc.scalar.activation(ab[:, :, :], abarg[:, :, :], ACT.Exp).then_inc(ab_done, 1)

                def step(S, half, ic, c, first, par, early):
                    if c == 0:
                        held(act, code_ld[0], (ic + 1) * 16)
                    mask(S, c, 0, 0, first)
                    mask(S, c, 0, 1, first)
                    pc = (c - 1) % n
                    if not first and pc > 0:
                        factors(ic if c > 0 else ic - 1, pc)
                    with act.Fori(1, NT // 4) as q:
                        mask(S, c, q, 0)
                        mask(S, c, q, 1)
                    if c == 0:
                        held(act, code_ld[1], (ic + 1) * 16)
                    with act.Fori(NT // 4, NT // 2) as q:
                        mask(S, c, q, 0)
                        mask(S, c, q, 1)
                    act.wait_ge(pe_quad, (S + 1) * (NT * NQ))
                    for b in range(6):
                        if not first:
                            act.wait_ge(acc_tr, (S - 1) * 6 + b + 1)
                        nc.scalar.activation(accS[:, b, :], ps[:, b, :], ACT.Copy).then_inc(acc_ev, 1)

                class_steps(act, kvals, step, lambda S, ic: factors(ic, n - 1))
            both_paths(act, "Activation", program)

        @block.vector
        def _(dve):
            link = Chain(dve, vstep)
            dve.wait_ge(ld_x, 16)
            layernorm(dve, link, xs[:, :, :], h0[:, :, :], sq0[:, :, :], 1)
            dve.wait_ge(w0T_ps, 1)
            nc.vector.tensor_copy(w0T[:, :], ps[0:F, 4, 0:F]).then_inc(w0T_sb, 1)
            dve.wait_ge(wa_ps, 1)
            nc.vector.tensor_copy(w0s[:, F:F + 2], ps[0:F, 5, 0:2]).then_inc(wa_sb, 1)
            nc.vector.tensor_copy(wrep[:, :], ps[0:F, 5, 0:1].to_broadcast([F, P])).then_inc(wa_sb, 1)
            for g in range(NI):
                dve.wait_ge(hT_ps, g + 1)
                nc.vector.tensor_copy(h0T[:, g * CH:(g + 1) * CH], ps[0:F, g % 4, :]).then_inc(hT_sb, 1)
            for g in range(NI):
                dve.wait_ge(wh_ps, g + 1)
                nc.vector.tensor_copy(wh[:, g * IB:(g + 1) * IB, :],
                                      ps[:, 4 + g % 4, 0:IB * (F + 2)].rearrange("p (t f) -> p t f", f=F + 2))\
                    .then_inc(wh_sb, 1)
            dve.wait_ge(wh_sb, NI)
            nc.vector.tensor_reduce(dm[:, 0:1], wh[:, :, F + 1], AX.X, ALU.max).then_inc(dmax_in, 1)
            nc.vector.tensor_reduce(whsum[:, :], wh[:, :, 0:F].rearrange("p t f -> p f t"), AX.X, ALU.add)\
                .then_inc(mean_in, 1)
            dve.wait_ge(dmax_out, 1)
            nc.vector.tensor_scalar(d0[:, :], wh[:, :, F + 1], dm[:, 1:2], None, ALU.subtract).then_inc(dshift, 1)
            for g in range(NI):
                dve.wait_ge(rrow_ps, g + 1)
                nc.vector.tensor_scalar(r0[:, g * CH:(g + 1) * CH], ps[:, g % 4, :], dm[:, 1:2], 0.0, ALU.add,
                                        ALU.max).then_inc(rrow_z, 1)
            dve.wait_ge(dexp, 2)
            nc.vector.tensor_tensor(W0e[:, :, 0:F], wh[:, :, 0:F], W0e[:, :, F:F + 1].to_broadcast([P, NT, F]),
                                    ALU.mult).then_inc(w0_ready, 1)
            dve.wait_ge(mean_ps, 1)
            nc.vector.tensor_copy(whmean[:, :], ps[:, 7, 0:F]).then_inc(mean_sb, 1)
            dve.wait_ge(rrow_done, NI)
            dve.wait_ge(mean_sb, 1)
            vbase = link.n
            FIN = 9
            with dve.Fori(0, NI) as ic:
                dve.wait_ge(code_st, ic * 16)
                for b in range(IB):
                    for g in range(NG):
                        m = (ic * IB + b) * NG + g
                        dve.wait_ge(tg_done, m + 1)
                        src = ps[:, g, :].bitcast(bf16).rearrange("p (t i) -> p t i", i=P)
                        nc.vector.tensor_scalar(code0[:, g * G8:(g + 1) * G8, b * P:(b + 1) * P], src, float(KC - 1),
                                                -1.0, ALU.min, ALU.max).then_inc(ev_done, 1)
                dve.wait_ge(pos_done, (ic + 1) * IB)
                for jt in range(NT):
                    if jt >= 4:
                        dve.wait_ge(t0_used, ic * NT + jt - 3)
                    else:
                        dve.wait_ge(t0_used, ic * NT)
                    nc.vector.scalar_tensor_tensor(out=T0[:, jt % 4, :], in0=r0[:, bass.ds(ic * CH, CH)],
                                                   scalar=th0[:, jt:jt + 1], in1=pos0[:, jt, :], op0=ALU.max,
                                                   op1=ALU.min).then_inc(t0_made, 1)
                dve.wait_ge(t0_used, (ic + 1) * NT)
                nc.vector.tensor_copy(A0s[:, :], ps[0:F + 1, 5, :]).then_inc(a0_sb, 1)
                dve.wait_ge(a0_tr, ic + 1)
                at = ps[:, 6, 0:IB * (F + 1)].rearrange("p (b f) -> p b f", f=F + 1)
                dn, pres, absent, rec = (den0[:, m, :] for m in range(4))

                def wide(a):
                    return a.unsqueeze(2).to_broadcast([P, IB, F])
                hv = h0[:, bass.ds(ic * IB, IB), :]
                mean_b = whmean[:, :].unsqueeze(1).to_broadcast([P, IB, F])
                seq = [lambda: nc.vector.tensor_copy(dn, at[:, :, F]),
                       lambda: nc.vector.tensor_scalar(pres, dn, 0.0, None, ALU.is_gt),
                       lambda: nc.vector.tensor_scalar(absent, pres, -1.0, 1.0, ALU.mult, ALU.add),
                       lambda: nc.vector.tensor_tensor(dn, dn, absent, ALU.add),
                       lambda: nc.vector.reciprocal(rec, dn),
                       lambda: nc.vector.tensor_tensor(rec, rec, pres, ALU.mult),
                       lambda: nc.vector.tensor_tensor(fin0[:, 0, :, :], at[:, :, 0:F], wide(rec), ALU.mult),
                       lambda: nc.vector.tensor_tensor(fin0[:, 1, :, :], mean_b, wide(absent), ALU.mult),
                       lambda: nc.vector.tensor_tensor(hv, fin0[:, 0, :, :], fin0[:, 1, :, :], ALU.add)]
                assert len(seq) == FIN
                for m, f in enumerate(seq):
                    f().then_inc(a0_fin, 1)
                    dve.wait_ge(a0_fin, ic * FIN + m + 1)
            dve.wait_ge(code_st, NI * 16)
            dve.wait_ge(flag_ps, 1)
            link(nc.vector.tensor_tensor(flagscr[:, :], ps[:, 4, 0:P], identF[:, :], ALU.mult))
            link(nc.vector.tensor_reduce(flagcol[:, 0:1], flagscr[:, :], AX.X, ALU.add))
            link(nc.vector.tensor_copy(flagcol[:, 1:2], ps[:, 4, P:P + 1]))
            nc.vector.tensor_tensor(flagcol[:, 2:3], flagcol[:, 0:1], flagcol[:, 1:2], ALU.not_equal)\
                .then_inc(flag_sum, 1)
            dve.wait_ge(flag_tot, 1)
            nc.vector.tensor_copy(flagi[:, :], flagcol[:, 3:4]).then_inc(flag_done, 1)
            nc.vector.tensor_scalar(sq1[:, :, :], h0[:, :, :], 0.0, None, ALU.min).then_inc(elu_in, 1)
            link(nc.vector.scalar_tensor_tensor(out=xs[:, :, :], in0=h0[:, :, :], scalar=0.0, in1=xs[:, :, :],
                                                op0=ALU.max, op1=ALU.add))
            dve.wait_ge(elu_exp, 1)
            link(nc.vector.scalar_tensor_tensor(out=xs[:, :, :], in0=sq1[:, :, :], scalar=-1.0, in1=xs[:, :, :],
                                                op0=ALU.add, op1=ALU.add))
            layernorm(dve, link, xs[:, :, :], h1[:, :, :], sq1[:, :, :], 2)
            link(nc.vector.memset(hT[F:F + 1, :], 1.0))
            link(nc.vector.memset(sa[:, KHV:KH], 0.0))
            link(nc.vector.memset(sbm[:, KHV:KH], 0.0))
            dve.wait_ge(wT_ps, 3)
            for dst, bank in ((qT, 4), (kT, 5)):
                nc.vector.tensor_copy(dst[:, :, :], ps[:, bank, 0:DC * (F + 1)].rearrange("p (c f) -> p c f", f=F + 1))\
                    .then_inc(wT_sb, 1)
            for hh in range(2):
                nc.vector.tensor_copy(vT[:, 4 * hh:4 * hh + 4, :],
                                      ps[0:F, 6 + hh, 0:4 * (F + 1)].rearrange("p (h f) -> p h f", f=F + 1))\
                    .then_inc(wT_sb, 1)
            for g in range(NI):
                dve.wait_ge(hT_ps, NI + g + 1)
                nc.vector.tensor_copy(hT[0:F, g * CH:(g + 1) * CH], ps[0:F, g % 4, :]).then_inc(hT_sb, 1)
            dve.wait_ge(s_ps, 1)
            nc.vector.tensor_copy(sa[:, 0:KHV], ps[0:F + 1, 4, 0:KHV]).then_inc(s_sb, 1)
            nc.vector.tensor_copy(sbm[:, 0:KHV], ps[0:F + 1, 5, 0:KHV]).then_inc(s_sb, 1)
            nc.vector.tensor_copy(vpw[:, :], ps[0:F + 1, 6, :]).then_inc(s_sb, 1)
            for g in range(NI):
                dve.wait_ge(bT_ps, g + 1)
                nc.vector.tensor_reduce(bm8[:, g:g + 1], ps[0:KH, g % 4, :], AX.X, ALU.max).then_inc(bT_red, 1)
            dve.wait_ge(bT_red, NI)
            link(nc.vector.tensor_reduce(bm8[:, NI:NI + 1], bm8[:, 0:NI], AX.X, ALU.max))
            nc.vector.tensor_copy(bmrep[:, :], bm8[:, NI:NI + 1].to_broadcast([KH, P])).then_inc(bmx_in, 1)
            dve.wait_ge(bmx_ps, 1)
            link(nc.vector.tensor_copy(bmx[:, :], ps[:, 7, 0:KH]))
            for g in range(NI):
                dve.wait_ge(aT_ps, g + 1)
                nc.vector.tensor_scalar(rT[:, g * CH:(g + 1) * CH], ps[0:KH, g % 4, :], bm8[:, NI:NI + 1], 0.0,
                                        ALU.add, ALU.max).then_inc(aT_z, 1)
            for g in range(2 * NI):
                dve.wait_ge(ab_ps, g + 1)
                t0 = (g % NI) * IB
                dst = (bt if g < NI else LL)[:, t0:t0 + IB, :]
                nc.vector.tensor_tensor(dst, ps[:, 4 + g % 3, 0:IB * KH].rearrange("p (t c) -> p t c", c=KH),
                                        bmx[:, :].unsqueeze(1).to_broadcast([P, IB, KH]),
                                        ALU.subtract if g < NI else ALU.add).then_inc(ab_sb, 1)
            dve.wait_ge(ab_sb, 2 * NI)
            nc.vector.tensor_scalar(bt[:, :, :], bt[:, :, :], 0.0, None, ALU.min).then_inc(tab_in, 1)
            link(nc.vector.scalar_tensor_tensor(out=LL[:, :, :], in0=LL[:, :, :], scalar=SLOPE, in1=LL[:, :, :],
                                                op0=ALU.mult, op1=ALU.max))
            dve.wait_ge(tab_in, 1)
            dve.sem_inc(pre_end, 1)
            dve.wait_ge(pre_end, 4)

            def program(kvals):
                n = len(kvals)

                def probs(S, c, par, q, u, early=False):
                    jt = q * 2 + u
                    num = S * NT + jt
                    dve.wait_ge(mask_made, num + 1)
                    for h in range(H):
                        if h % 4 == 0 and not early:
                            dve.wait_ge(pe_quad, (num - 1) * NQ + h // 4 + 1)
                        last = nc.vector.scalar_tensor_tensor(
                            out=T[:, h, :], in0=R[:, par, h, :],
                            scalar=th[:, bass.ds(jt, 1), c * H + h:c * H + h + 1].rearrange("p a b -> p (a b)"),
                            in1=M[:, u, :], op0=ALU.max, op1=ALU.mult)
                        if h % 4 == 3:
                            last.then_inc(t_made, 1)

                def recip(S, ic):
                    dve.wait_ge(den_fin, ic + 1)
                    nc.vector.reciprocal(rden[:, :], den[:, :]).then_inc(rden_ok, 1)

                def step(S, half, ic, c, first, par, early):
                    dve.wait_ge(r_ld[par], (half + 1) * 16)
                    probs(S, c, par, 0, 0, first)
                    probs(S, c, par, 0, 1)
                    with dve.Fori(1, 7) as q:
                        probs(S, c, par, q, 0)
                        probs(S, c, par, q, 1)
                    if c == 0 and not first:
                        recip(S, ic - 1)
                    with dve.Fori(7, NT // 2) as q:
                        probs(S, c, par, q, 0)
                        probs(S, c, par, q, 1)
                    if not first:
                        dve.wait_ge(merged, S * (3 * 2 * IB))
                    for b in range(6):
                        dve.wait_ge(acc_tr, S * 6 + b + 1)
                        sp_ = ps[:, 6 + b % 2, :].rearrange("p (b c) -> p b c", b=IB)
                        if b % 3 < 2:
                            pair = (b // 3) * 2 + b % 3
                            nc.vector.tensor_copy(accT[:, :, 2 * pair:2 * pair + 2, :],
                                                  sp_.rearrange("p b (h f) -> p b h f", f=F)).then_inc(accT_done, 1)
                        else:
                            nc.vector.tensor_copy(denT[:, :, (b // 3) * 4:(b // 3) * 4 + 4],
                                                  sp_.rearrange("p b (h r) -> p b h r", r=32)[:, :, :, 0])\
                                .then_inc(accT_done, 1)

                class_steps(dve, kvals, step, lambda S, ic: recip(S, ic))
            both_paths(dve, "DVE", program)

        @block.tensor
        def _(pe):
            pe.wait_ge(consts, 6 + CL)
            pe.wait_ge(ld_w0, 48)
            nc.tensor.transpose(ps[0:F, 4, 0:F], w0s[:, 0:F], identF[0:F, 0:F]).then_inc(w0T_ps, 1)
            pe.wait_ge(w0T_sb, 1)
            nc.tensor.matmul(ps[0:F, 5, 0:2], w0T[:, :], a0s[:, :], start=True, stop=True).then_inc(wa_ps, 1)

            def transposed(src, done, base):
                for g in range(NI):
                    if base + g >= 4:
                        pe.wait_ge(hT_sb, base + g - 3)
                    for b in range(IB):
                        last = nc.tensor.transpose(ps[0:F, g % 4, b * P:(b + 1) * P], src[:, g * IB + b, :],
                                                   identF[:, :])
                    last.then_inc(hT_ps, 1)
            pe.wait_ge(ln_done, 1)
            transposed(h0, ln_done, 0)
            pe.wait_ge(wa_sb, 2)
            for g in range(NI):
                pe.wait_ge(hT_sb, g + 1)
                if g >= 4:
                    pe.wait_ge(wh_sb, g - 3)
                for b in range(IB):
                    t = g * IB + b
                    last = nc.tensor.matmul(ps[:, 4 + g % 4, b * (F + 2):(b + 1) * (F + 2)],
                                            h0T[:, t * P:(t + 1) * P], w0s[:, :], start=True, stop=True)
                last.then_inc(wh_ps, 1)
            for g in range(NI):
                if g >= 4:
                    pe.wait_ge(rrow_z, g - 3)
                nc.tensor.matmul(ps[:, g % 4, :], wrep[:, :], h0T[:, g * CH:(g + 1) * CH], start=True, stop=True)\
                    .then_inc(rrow_ps, 1)
            pe.wait_ge(mean_in, 1)
            pe.wait_ge(wh_sb, NI)
            nc.tensor.matmul(ps[:, 7, 0:F], meanmat[:, :], whsum[:, :], start=True, stop=True).then_inc(mean_ps, 1)
            pe.wait_ge(w0_ready, 1)
            pe.wait_ge(rrow_z, NI)
            nc.tensor.matmul(ps[:, 4, 0:P + 1], zerosB[:, 0:P], zerosB[:, :], start=True, stop=False,
                             skip_group_check=True)
            pe.sem_inc(blk_done, 1)
            with pe.Fori(0, NI) as ic:
                for b in range(IB):
                    pe.wait_ge(cast_done, ic * IB + b + 2)
                    for g in range(NG):
                        if b > 0:
                            pe.wait_ge(ev_done, (ic * IB + b - 1) * NG + g + 1)
                        for e in range(G8):
                            j = (g * G8 + e) * P
                            blk = abf[:, b % 2, j:j + P]
                            dst = ps[:, g, :].bitcast(bf16)[:, e * P:(e + 1) * P]
                            last = nc.tensor.transpose(dst, blk, identB[:, :])
                            nc.tensor.matmul(ps[:, 4, 0:P], blk, blk, start=False, stop=False, skip_group_check=True)
                            summed = nc.tensor.matmul(ps[:, 4, P:P + 1], blk, onesB[:, :], start=False, stop=False,
                                                      skip_group_check=True)
                        last.then_inc(tg_done, 1)
                    summed.then_inc(blk_done, 1)
                for jt in range(NT):
                    pe.wait_ge(t0_made, ic * NT + jt + 1)
                    nc.tensor.matmul(ps[0:F + 1, 5, :], W0e[:, jt, :], T0[:, jt % 4, :], start=(jt == 0),
                                     stop=(jt == NT - 1)).then_inc(t0_used, 1)
                pe.wait_ge(a0_sb, ic + 1)
                for b in range(IB):
                    last = nc.tensor.transpose(ps[:, 6, b * (F + 1):(b + 1) * (F + 1)], A0s[:, b * P:(b + 1) * P],
                                               identF[0:F + 1, 0:F + 1])
                last.then_inc(a0_tr, 1)
            nc.tensor.matmul(ps[:, 4, 0:P + 1], zerosB[:, 0:P], zerosB[:, :], start=False, stop=True,
                             skip_group_check=True).then_inc(flag_ps, 1)
            pe.wait_ge(ld_l1, 16 * (6 + KC + 2))
            pe.wait_ge(flag_sum, 1)
            pe.wait_ge(a0_fin, NI * 9)
            for w, bank in ((qw, 4), (kw, 5)):
                for c in range(DC):
                    last = nc.tensor.transpose(ps[:, bank, c * (F + 1):(c + 1) * (F + 1)], w[:, c * P:(c + 1) * P],
                                               identF[0:F + 1, 0:F + 1])
                last.then_inc(wT_ps, 1)
            for h in range(H):
                last = nc.tensor.transpose(ps[0:F, 6 + h // 4, (h % 4) * (F + 1):(h % 4 + 1) * (F + 1)],
                                           vw[:, h * F:(h + 1) * F], identF[0:F + 1, 0:F + 1])
            last.then_inc(wT_ps, 1)
            pe.wait_ge(wT_sb, 4)
            for w, bank, half in ((qT, 4, 0), (kT, 5, 1)):
                for c in range(DC):
                    nc.tensor.matmul(ps[0:F + 1, bank, 0:KHV], w[:, c, :],
                                     av[:, half * DC + c, :, :].rearrange("p k h -> p (k h)"), start=(c == 0),
                                     stop=(c == DC - 1))
            for h in range(H):
                last = nc.tensor.matmul(ps[0:F + 1, 6, h * F:(h + 1) * F], vT[:, h, :], pw[:, h, :], start=True,
                                        stop=True)
            last.then_inc(s_ps, 1)
            pe.wait_ge(ln_done, 2)
            transposed(h1, ln_done, NI)
            pe.wait_ge(hT_sb, 2 * NI)
            pe.wait_ge(s_sb, 3)
            for g in range(NI):
                if g >= 4:
                    pe.wait_ge(bT_red, g - 3)
                nc.tensor.matmul(ps[0:KH, g % 4, :], sbm[:, :], hT[:, g * CH:(g + 1) * CH], start=True, stop=True)\
                    .then_inc(bT_ps, 1)
            pe.wait_ge(bmx_in, 1)
            nc.tensor.matmul(ps[:, 7, 0:KH], bmrep[:, :], identF[0:KH, 0:KH], start=True, stop=True).then_inc(bmx_ps, 1)
            for g in range(NI):
                if g >= 4:
                    pe.wait_ge(aT_z, g - 3)
                nc.tensor.matmul(ps[0:KH, g % 4, :], sa[:, :], hT[:, g * CH:(g + 1) * CH], start=True, stop=True)\
                    .then_inc(aT_ps, 1)
            for g in range(2 * NI):
                if g >= 3:
                    pe.wait_ge(ab_sb, g - 2)
                for b in range(IB):
                    t = (g % NI) * IB + b
                    last = nc.tensor.matmul(ps[:, 4 + g % 3, b * KH:(b + 1) * KH], hT[:, t * P:(t + 1) * P],
                                            (sbm if g < NI else sa)[:, :], start=True, stop=True)
                last.then_inc(ab_ps, 1)
            pe.wait_ge(ab_sb, 2 * NI)
            for t in range(NT):
                if t >= 4:
                    pe.wait_ge(vp_sb, t - 3)
                nc.tensor.matmul(ps[:, 4 + t % 4, :], hT[:, t * P:(t + 1) * P], vpw[:, :], start=True, stop=True)\
                    .then_inc(vp_ps, 1)
            pe.wait_ge(vp_sb, NT)
            pe.wait_ge(aT_z, NI)
            pe.wait_ge(rT_st, 16)
            pe.sem_inc(pre_end, 2)
            pe.wait_ge(pre_end, 4)

            def program(kvals):
                n = len(kvals)

                def products(S, q, u, begin, end, first=False):
                    jt = q * 2 + u
                    num = S * NT + jt
                    pe.wait_ge(w_staged, (num + 1) * 2)
                    for Q in range(NQ):
                        pe.wait_ge(t_made, num * NQ + Q + 1)
                        if begin and not first:
                            pe.wait_ge(acc_ev, (S - 1) * 6 + 3 * Q + 3)
                        for hh in range(4):
                            h = 4 * Q + hh
                            p0 = F * (hh % 2)
                            nc.tensor.matmul(ps[p0:p0 + F, 3 * Q + hh // 2, :], Ws[:, u, h, :], T[:, h, :],
                                             start=begin, stop=end)
                        for hh in range(4):
                            h = 4 * Q + hh
                            last = nc.tensor.matmul(ps[32 * hh:32 * hh + 32, 3 * Q + 2, :], Ds[:, u, h, :], T[:, h, :],
                                                    start=begin, stop=end, tile_position=(0, 32 * hh))
                        last.then_inc(pe_quad, 1)

                def step(S, half, ic, c, first, par, early):
                    products(S, 0, 0, True, False, first)
                    products(S, 0, 1, False, False)
                    with pe.Fori(1, NT // 2 - 1) as q:
                        products(S, q, 0, False, False)
                        products(S, q, 1, False, False)
                    products(S, NT // 2 - 1, 0, False, False)
                    products(S, NT // 2 - 1, 1, False, True)
                    for b in range(6):
                        pe.wait_ge(acc_ev, S * 6 + b + 1)
                        if not (first and b < 2):
                            pe.wait_ge(accT_done, S * 6 + b - 1)
                        for i in range(IB):
                            last = nc.tensor.transpose(ps[:, 6 + b % 2, i * P:(i + 1) * P],
                                                       accS[:, b, i * P:(i + 1) * P], identF[:, :])
                        last.then_inc(acc_tr, 1)

                class_steps(pe, kvals, step, lambda S, ic: None)
            both_paths(pe, "PE", program)


_INS = ['x', 'adj', 'L0_gnn_W', 'L0_gnn_a', 'L1_gnn_Qw', 'L1_gnn_Qb', 'L1_gnn_Kw', 'L1_gnn_Kb', 'L1_gnn_Vw',
        'L1_gnn_Vb', 'L1_gnn_a', 'L1_gnn_Pw', 'L1_gnn_Pb']


def kernel(**inputs):
    import numpy as _np
    import concourse.bacc as _bacc
    from concourse import mybir as _mybir
    from concourse.bass_utils import run_bass_kernel_spmd as _run

    nc = _bacc.Bacc("TRN2", target_bir_lowering=False, num_devices=1)
    arrays, args = {}, []
    for name in _INS:
        a = _np.ascontiguousarray(inputs[name])
        arrays[f"in_{name}"] = a
        args.append(nc.dram_tensor(f"in_{name}", a.shape, _mybir.dt.from_np(a.dtype), kind="ExternalInput").ap())
    shape = arrays["in_x"].shape
    out = nc.dram_tensor("out_0", shape, _mybir.dt.float32, kind="ExternalOutput").ap()
    two_layer_graph_attention(nc, *args, out)
    r = _run(nc, [arrays], core_ids=[0])
    return r.results[0]["out_0"]
```

```python
from contextlib import ExitStack

import concourse.bass as bass
from concourse import mybir


def two_layer_graph_attention(nc, x, adj, W0, a0, Qw, Qb, Kw, Kb, Vw, Vb, a1, Pw, Pb, out):
    f32 = mybir.dt.float32
    bf16 = mybir.dt.bfloat16
    i8 = mybir.dt.int8
    i32 = mybir.dt.int32
    ALU = mybir.AluOpType
    ACT = mybir.ActivationFunctionType
    AX = mybir.AxisListType

    N, F = x.shape
    P = 128
    NT = N // P
    CH = 512
    NI = N // CH
    IB = CH // P
    KC, _, H = a1.shape
    HD = H * F
    CL = KC + 1
    KH = CL * H
    KHV = KC * H
    DC = HD // P
    NQ = H // 4
    G8 = 8
    NG = NT // G8
    SLOPE = 0.2
    EPS = 1e-5
    ABSENT = 1e30

    x_v = x.rearrange("(t p) f -> p t f", p=P)
    out_v = out.rearrange("(t p) f -> p t f", p=P)
    adj_v = adj.rearrange("(m p) j -> m p j", p=P)
    code_dram = nc.dram_tensor("code_scratch", (NI * P, NT * CH), i8).ap()
    x1_dram = nc.dram_tensor("x1_scratch", (NI * P, IB * F), f32).ap()
    shift_dram = nc.dram_tensor("shift_scratch", (NI * P, IB * KH), f32).ap()
    r_dram = nc.dram_tensor("r_scratch", (KH, N), f32).ap()

    ctx = ExitStack()
    with ctx:
        def sem(name):
            return ctx.enter_context(nc.semaphore(name))

        def sb(scope, name, shape, dt):
            return scope.enter_context(nc.sbuf_tensor(name, shape, dt))

        identF = sb(ctx, "identF", [P, P], f32)
        onesF = sb(ctx, "onesF", [P, 1], f32)
        pb = sb(ctx, "pb", [P, F], f32)
        classneg = sb(ctx, "classneg", [P, CL], f32)
        flagi = sb(ctx, "flagi", [P, 1], i32)

        wsc = ExitStack()
        qw = sb(wsc, "qw", [F + 1, HD], f32)
        kw = sb(wsc, "kw", [F + 1, HD], f32)
        vw = sb(wsc, "vw", [F + 1, HD], f32)
        av = sb(wsc, "av", [P, 2 * DC, KC, H], f32)
        pw = sb(wsc, "pw", [F, H, F], f32)
        meanmat = sb(wsc, "meanmat", [P, P], f32)
        zerosB = sb(wsc, "zerosB", [P, P + 1], bf16)
        flagscr = sb(wsc, "flagscr", [P, P], f32)
        identB = sb(wsc, "identB", [P, P], bf16)
        onesB = sb(wsc, "onesB", [P, 1], bf16)
        stat = sb(wsc, "stat", [P, 5, NT], f32)
        flagcol = sb(wsc, "flagcol", [P, 4], f32)
        xs = sb(wsc, "xs", [P, NT, F], f32)
        h0 = sb(wsc, "h0", [P, NT, F], f32)

        l0 = ExitStack()
        raw = sb(l0, "raw", [P, IB, N], i32)
        abf = sb(l0, "abf", [P, 2, N], bf16)
        code0 = sb(l0, "code0", [P, NT, CH], i8)
        pos0 = sb(l0, "pos0", [P, NT, CH], i8)
        r0 = sb(l0, "r0", [P, N], f32)
        share0 = sb(l0, "share0", [P, N], f32)
        sq0 = share0[:, 0:NT * F].rearrange("p (t f) -> p t f", f=F)
        h0T = share0[0:F, :]
        T0 = share0[:, 0:4 * CH].rearrange("p (s i) -> p s i", i=CH)
        wh = sb(l0, "wh", [P, NT, F + 2], f32)
        w0s = sb(l0, "w0s", [F, F + 2], f32)
        w0T = sb(l0, "w0T", [F, F], f32)
        a0s = sb(l0, "a0s", [F, 2], f32)
        wrep = sb(l0, "wrep", [F, P], f32)
        W0e = sb(l0, "W0e", [P, NT, F + 1], f32)
        th0 = sb(l0, "th0", [P, NT], f32)
        d0 = sb(l0, "d0", [P, NT], f32)
        dm = sb(l0, "dm", [P, 4], f32)
        whsum = sb(l0, "whsum", [P, F], f32)
        whmean = sb(l0, "whmean", [P, F], f32)
        A0s = sb(l0, "A0s", [F + 1, CH], f32)
        fin0 = sb(l0, "fin0", [P, 4, IB, F], f32)
        den0 = sb(l0, "den0", [P, 4, IB], f32)
        l0.close()
        wsc.close()

        l1 = ExitStack()
        vp = sb(l1, "vp", [P, NT, HD], f32)
        th = sb(l1, "th", [P, NT, KH], f32)
        dd = sb(l1, "dd", [P, NT, KH], f32)
        code = sb(l1, "code", [P, NT, CH], i8)
        pre = ExitStack()
        LL = sb(pre, "LL", [P, NT, KH], f32)
        hT = sb(pre, "hT", [F + 1, N], f32)
        rT = sb(pre, "rT", [KH, N], f32)
        h1 = sb(pre, "h1", [P, NT, F], f32)
        sq1 = sb(pre, "sq1", [P, NT, F], f32)
        bt = sb(pre, "bt", [P, NT, KH], f32)
        qT = sb(pre, "qT", [P, DC, F + 1], f32)
        kT = sb(pre, "kT", [P, DC, F + 1], f32)
        vT = sb(pre, "vT", [F, H, F + 1], f32)
        sa = sb(pre, "sa", [F + 1, KH], f32)
        sbm = sb(pre, "sbm", [F + 1, KH], f32)
        vpw = sb(pre, "vpw", [F + 1, HD], f32)
        bm8 = sb(pre, "bm8", [KH, NI + 1], f32)
        bmrep = sb(pre, "bmrep", [KH, P], f32)
        bmx = sb(pre, "bmx", [P, KH], f32)
        pre.close()
        R = sb(l1, "R", [P, 2, H, CH], f32)
        T = sb(l1, "T", [P, 2, H, CH], f32)
        x1c = sb(l1, "x1c", [P, IB, F], f32)
        shift = sb(l1, "shift", [P, IB, KH], f32)
        Ws = sb(l1, "Ws", [P, 2, H, F], f32)
        Ds = sb(l1, "Ds", [P, 2, H, 32], f32)
        Mt = sb(l1, "Mt", [P, 2, CH], bf16)
        M = sb(l1, "M", [P, 2, CH], bf16)
        accS = sb(l1, "accS", [P, 6, CH], f32)
        accT = sb(l1, "accT", [P, IB, H, F], f32)
        O = sb(l1, "O", [P, IB, H, F], f32)
        tmp = sb(l1, "tmp", [P, H, F], f32)
        denT = sb(l1, "denT", [P, IB, H], f32)
        tiny = sb(l1, "tiny", [P, 4, IB * H], f32)
        abarg = sb(l1, "abarg", [P, 2, IB * H], f32)
        ab = sb(l1, "ab", [P, 2, IB * H], f32)
        cst = sb(l1, "cst", [P, IB * H], f32)
        den = sb(l1, "den", [P, IB * H], f32)
        rden = sb(l1, "rden", [P, IB * H], f32)
        res = sb(l1, "res", [P, IB, F], f32)
        l1.close()

        ps = ctx.enter_context(nc.psum_tensor("ps", [P, 8, CH], f32))

        ld_x, ld_w0, ld_l1 = sem("ld_x"), sem("ld_w0"), sem("ld_l1")
        consts = sem("consts")
        vstep, astep, pstep = sem("vstep"), sem("astep"), sem("pstep")
        ln_var, ln_std, ln_done = sem("ln_var"), sem("ln_std"), sem("ln_done")
        hT_ps, hT_sb = sem("hT_ps"), sem("hT_sb")
        w0T_ps, w0T_sb, wa_ps, wa_sb = sem("w0T_ps"), sem("w0T_sb"), sem("wa_ps"), sem("wa_sb")
        wh_ps, wh_sb = sem("wh_ps"), sem("wh_sb")
        dmax_in, dmax_out, dshift, dexp = sem("dmax_in"), sem("dmax_out"), sem("dshift"), sem("dexp")
        rrow_ps, rrow_z, rrow_done = sem("rrow_ps"), sem("rrow_z"), sem("rrow_done")
        w0_ready, mean_in, mean_ps, mean_sb = sem("w0_ready"), sem("mean_in"), sem("mean_ps"), sem("mean_sb")
        raw_ld = [sem(f"raw_ld{b}") for b in range(IB)]
        cast_done, blk_done, tg_done, ev_done = sem("cast_done"), sem("blk_done"), sem("tg_done"), sem("ev_done")
        pos_done, code_st = sem("pos_done"), sem("code_st")
        t0_made, t0_used = sem("t0_made"), sem("t0_used")
        a0_sb, a0_tr, a0_fin = sem("a0_sb"), sem("a0_tr"), sem("a0_fin")
        flag_ps, flag_sum, flag_tot, flag_done = sem("flag_ps"), sem("flag_sum"), sem("flag_tot"), sem("flag_done")
        elu_in, elu_exp = sem("elu_in"), sem("elu_exp")
        l0_end = sem("l0_end")
        wT_ps, wT_sb, s_ps, s_sb = sem("wT_ps"), sem("wT_sb"), sem("s_ps"), sem("s_sb")
        bT_ps, bT_red, bmx_in, bmx_ps, bmx_sb = sem("bT_ps"), sem("bT_red"), sem("bmx_in"), sem("bmx_ps"), sem("bmx_sb")
        ab_ps, ab_sb, aT_ps, aT_z, rT_done, rT_st = (sem("ab_ps"), sem("ab_sb"), sem("aT_ps"), sem("aT_z"),
                                                   sem("rT_done"), sem("rT_st"))
        tab_in, tab_exp, vp_ps, vp_sb = sem("tab_in"), sem("tab_exp"), sem("vp_ps"), sem("vp_sb")
        pre_end, x1_st, shift_ok, shift_st = sem("pre_end"), sem("x1_st"), sem("shift_ok"), sem("shift_st")
        x1_ld, shift_ld = sem("x1_ld"), sem("shift_ld")
        r_ld = [sem("r_ld0"), sem("r_ld1")]
        code_ld = [sem("code_ld0"), sem("code_ld1")]
        abs_done, mask_made, t_made, pe_quad = sem("abs_done"), sem("mask_made"), sem("t_made"), sem("pe_quad")
        w_staged, acc_ev, acc_tr, accT_done = sem("w_staged"), sem("acc_ev"), sem("acc_tr"), sem("accT_done")
        ab_arg, ab_done, merged, den_fin, rden_ok = (sem("ab_arg"), sem("ab_done"), sem("merged"), sem("den_fin"),
                                                    sem("rden_ok"))
        mstep, fstep = sem("mstep"), sem("fstep")
        out_st = sem("out_st")
        passed = sem("passed")

        class Chain:

            def __init__(self, eng, s):
                self.eng, self.s, self.n = eng, s, 0

            def __call__(self, ins):
                self.n += 1
                ins.then_inc(self.s, 1)
                self.eng.wait_ge(self.s, self.n)

        def held(eng, s, value):
            eng.wait_ge(s, value)
            eng.sem_inc(passed, 1)

        def layernorm(dve, link, src, cen, sq, which):
            s, mean, v, rr, t = (stat[:, n, :] for n in range(5))

            def wide(a):
                return a.unsqueeze(2).to_broadcast([P, NT, F])
            link(nc.vector.tensor_reduce(s, src, AX.X, ALU.add))
            link(nc.vector.tensor_scalar(mean, s, 1.0 / F, None, ALU.mult))
            link(nc.vector.tensor_tensor(cen, src, wide(mean), ALU.subtract))
            link(nc.vector.tensor_tensor(sq, cen, cen, ALU.mult))
            link(nc.vector.tensor_reduce(s, sq, AX.X, ALU.add))
            nc.vector.tensor_scalar(v, s, 1.0 / F, EPS, ALU.mult, ALU.add).then_inc(ln_var, 1)
            dve.wait_ge(ln_var, which)
            dve.wait_ge(ln_std, which)
            link(nc.vector.reciprocal(rr, t))
            link(nc.vector.tensor_tensor(t, rr, rr, ALU.mult))
            link(nc.vector.tensor_tensor(t, t, v, ALU.mult))
            link(nc.vector.tensor_scalar(t, t, -0.5, 1.5, ALU.mult, ALU.add))
            link(nc.vector.tensor_tensor(rr, rr, t, ALU.mult))
            nc.vector.scalar_tensor_tensor(out=cen, in0=cen, scalar=0.0, in1=wide(rr), op0=ALU.max,
                                           op1=ALU.mult).then_inc(ln_done, 1)
            dve.wait_ge(ln_done, which)

        def class_steps(eng, kvals, step, tail):
            n = len(kvals)
            u = 1 if n % 2 == 0 else 2

            def body(I, peeled):
                for e in range(u):
                    for c in range(n):
                        s = e * n + c
                        step(I * (u * n) + s, I * (u * n // 2) + s // 2, I * u + e, c, peeled and s == 0,
                             s % 2, peeled and s < 2)
            body(0, True)
            with eng.Fori(1, NI // u) as I:
                body(I, False)
            tail(NI * n, NI - 1)

        def both_paths(eng, engine_type, program):
            eng.wait_ge(flag_done, 1)
            flag = eng.value_load(flagi[0:1, 0:1], min_val=0, max_val=1)
            with eng.If(flag < 1):
                program([0, 1])
            with eng.Else():
                program(list(range(KC)) + [-1])

        block = ctx.enter_context(nc.Block())

        @block.sync
        def _(sp):
            sp.dma_start(xs[:, :, :], x_v).then_inc(ld_x, 16)
            sp.dma_start(w0s[:, 0:F], W0).then_inc(ld_w0, 16)
            for half in range(2):
                sp.dma_start(a0s[:, half:half + 1], a0[half * F:(half + 1) * F, :]).then_inc(ld_w0, 16)
            with sp.Fori(0, NI) as ic:
                for b in range(IB):
                    sp.wait_ge(cast_done, ic * IB + b + 1)
                    sp.dma_start(raw[:, b, :], adj_v[bass.ds(ic * IB + b, 1), :, :].rearrange("a p j -> p (a j)"))\
                        .then_inc(raw_ld[b], 16)
            sp.wait_ge(ln_done, 2)
            sp.dma_start(x1_dram.rearrange("(c p) f -> p c f", p=P),
                         xs[:, :, :].rearrange("p (c b) f -> p c (b f)", b=IB)).then_inc(x1_st, 16)
            sp.wait_ge(rT_done, NI)
            sp.dma_start(r_dram, rT[:, :]).then_inc(rT_st, 16)
            sp.wait_ge(shift_ok, 1)
            sp.dma_start(shift_dram.rearrange("(c p) f -> p c f", p=P),
                         LL[:, :, :].rearrange("p (c b) k -> p c (b k)", b=IB)).then_inc(shift_st, 16)
            sp.wait_ge(x1_st, 16)
            sp.wait_ge(rT_st, 16)
            sp.wait_ge(shift_st, 16)
            sp.wait_ge(code_st, 16 * NI)
            sp.sem_inc(pre_end, 1)
            sp.wait_ge(pre_end, 5)

            def program(kvals):
                n = len(kvals)

                def step(S, half, ic, c, first, par, early):
                    if not early:
                        sp.wait_ge(t_made, (S - 1) * (NT * NQ))
                    k = c
                    sp.dma_start(R[:, par, :, :],
                                 r_dram[k * H:(k + 1) * H, bass.ds(ic * CH, CH)].partition_broadcast(P))\
                        .then_inc(r_ld[par], 16)
                    if c == 0:
                        for hf in range(2):
                            if not first:
                                held(sp, mask_made, S * NT - (1 - hf) * (NT // 2))
                            w = NT // 2
                            sp.dma_start(code[:, hf * w:(hf + 1) * w, :],
                                         code_dram[bass.ds(ic * P, P), hf * w * CH:(hf + 1) * w * CH]
                                         .rearrange("p (t i) -> p t i", t=w)).then_inc(code_ld[hf], 16)

                class_steps(sp, kvals, step, lambda S, ic: None)
            both_paths(sp, "SP", program)

        @block.gpsimd
        def _(pool):
            link = Chain(pool, pstep)
            link(nc.gpsimd.memset(identF[:, :], 0.0))
            link(nc.gpsimd.memset(identB[:, :], 0.0))
            for m in (identF, identB):
                nc.gpsimd.affine_select(out=m[:, :], in_=m[:, :], compare_op=ALU.not_equal, fill=1.0, base=0,
                                        pattern=[[-1, P]], channel_multiplier=1).then_inc(consts, 1)
            nc.gpsimd.memset(meanmat[:, :], 1.0 / N).then_inc(consts, 1)
            nc.gpsimd.memset(zerosB[:, :], 0.0).then_inc(consts, 1)
            nc.gpsimd.memset(onesB[:, :], 1.0).then_inc(consts, 1)
            nc.gpsimd.memset(onesF[:, :], 1.0).then_inc(consts, 1)
            for c in range(CL):
                nc.gpsimd.memset(classneg[:, c:c + 1], float(-c if c < KC else 1)).then_inc(consts, 1)
            pool.wait_ge(dmax_in, 1)
            nc.gpsimd.partition_all_reduce(dm[:, 1:2], dm[:, 0:1], P, bass.bass_isa.ReduceOp.max)\
                .then_inc(dmax_out, 1)
            with pool.Fori(0, NI) as ic:
                held(pool, ev_done, (ic + 1) * (IB * NG))
                pool.dma_start(code_dram[bass.ds(ic * P, P), :], code0[:, :, :].rearrange("p t i -> p (t i)"))\
                    .then_inc(code_st, 16)
            pool.wait_ge(flag_sum, 1)
            nc.gpsimd.partition_all_reduce(flagcol[:, 3:4], flagcol[:, 2:3], P, bass.bass_isa.ReduceOp.max)\
                .then_inc(flag_tot, 1)
            pool.wait_ge(pre_end, 5)
            pbase = link.n

            def program(kvals):
                n = len(kvals)

                def stage(S, c, q, u, early=False):
                    jt = q * 2 + u
                    if not early:
                        held(pool, pe_quad, (S * NT + jt - 1) * NQ)
                    dj = dd[:, bass.ds(jt, 1), c * H:(c + 1) * H].rearrange("p a h -> p (a h)")
                    nc.gpsimd.tensor_tensor(Ws[:, u, :, :],
                                            vp[:, bass.ds(jt, 1), :].rearrange("p a (h f) -> p (a h) f", h=H),
                                            dj.unsqueeze(2).to_broadcast([P, H, F]), ALU.mult).then_inc(w_staged, 1)
                    nc.gpsimd.tensor_copy(Ds[:, u, :, :], dj.unsqueeze(2).to_broadcast([P, H, 32]))\
                        .then_inc(w_staged, 1)

                PER = 3 * 2 * IB
                CSTEPS = 20

                def scales(S, ic, c):
                    held(pool, accT_done, S * 6)
                    held(pool, shift_ld, (ic + 1) * 16)
                    L = shift[:, :, c * H:(c + 1) * H]
                    dT = denT[:, :, :].rearrange("p b h -> p (b h)")
                    pres, t1, t2, Lp = (tiny[:, m, :] for m in range(4))
                    base = (S - 1) * CSTEPS

                    def wide(a):
                        return a.rearrange("p (b h) -> p b h", h=H)
                    seq = [lambda: nc.gpsimd.tensor_scalar(pres, dT, 0.0, 1.0, ALU.is_gt, ALU.mult),
                           lambda: nc.gpsimd.tensor_tensor(wide(t1), L, wide(pres), ALU.mult),
                           lambda: nc.gpsimd.tensor_scalar(t2, pres, ABSENT, -ABSENT, ALU.mult, ALU.add),
                           lambda: nc.gpsimd.tensor_tensor(Lp, t1, t2, ALU.add)]
                    if c == 0:
                        seq += [lambda: nc.gpsimd.tensor_copy(cst[:, :], Lp),
                                lambda: nc.gpsimd.tensor_copy(den[:, :], dT)]
                    else:
                        seq += [lambda: nc.gpsimd.tensor_tensor(t1, Lp, cst[:, :], ALU.subtract),
                                lambda: nc.gpsimd.tensor_scalar(t1, t1, 0.0, 1.0, ALU.is_gt, ALU.mult),
                                lambda: nc.gpsimd.tensor_scalar(t2, t1, -1.0, 1.0, ALU.mult, ALU.add),
                                lambda: nc.gpsimd.tensor_tensor(t1, t1, Lp, ALU.mult),
                                lambda: nc.gpsimd.tensor_tensor(t2, t2, cst[:, :], ALU.mult),
                                lambda: nc.gpsimd.tensor_tensor(t1, t1, t2, ALU.add),
                                lambda: nc.gpsimd.tensor_tensor(abarg[:, 0, :], cst[:, :], t1, ALU.subtract),
                                lambda: nc.gpsimd.tensor_tensor(abarg[:, 1, :], Lp, t1, ALU.subtract),
                                lambda: nc.gpsimd.tensor_copy(cst[:, :], t1)]
                    for m, f in enumerate(seq):
                        f().then_inc(mstep, 1)
                        held(pool, mstep, base + m + 1)
                    m = len(seq)
                    if c > 0:
                        pool.sem_inc(ab_arg, 1)
                        held(pool, ab_done, ic * (n - 1) + c)
                        for f in (lambda: nc.gpsimd.tensor_tensor(den[:, :], den[:, :], ab[:, 0, :], ALU.mult),
                                  lambda: nc.gpsimd.tensor_tensor(t2, dT, ab[:, 1, :], ALU.mult),
                                  lambda: nc.gpsimd.tensor_tensor(den[:, :], den[:, :], t2, ALU.add)):
                            f().then_inc(mstep, 1)
                            m += 1
                            held(pool, mstep, base + m)
                    pool.sem_inc(mstep, CSTEPS - m)
                    if c == n - 1:
                        pool.sem_inc(den_fin, 1)

                def merge(S, c, piece, count):
                    A = accT[:, :, :, :].rearrange("p b (q h) f -> p (b q) h f", q=NQ)[:, bass.ds(piece, 1), :, :]\
                        .rearrange("p a h f -> p (a h) f")
                    Oq = O[:, :, :, :].rearrange("p b (q h) f -> p (b q) h f", q=NQ)[:, bass.ds(piece, 1), :, :]\
                        .rearrange("p a h f -> p (a h) f")

                    def factor(w):
                        return ab[:, w, :].rearrange("p (a h) -> p a h", h=4)[:, bass.ds(piece, 1), :]\
                            .rearrange("p a h -> p (a h)").unsqueeze(2).to_broadcast([P, 4, F])
                    if c == 0:
                        nc.gpsimd.tensor_copy(Oq, A).then_inc(merged, 1)
                        held(pool, merged, count + 1)
                        pool.sem_inc(merged, 2)
                        return
                    tq = tmp[:, 0:4, :]
                    nc.gpsimd.tensor_tensor(tq, A, factor(1), ALU.mult).then_inc(merged, 1)
                    nc.gpsimd.tensor_tensor(Oq, Oq, factor(0), ALU.mult).then_inc(merged, 1)
                    held(pool, merged, count + 2)
                    nc.gpsimd.tensor_tensor(Oq, Oq, tq, ALU.add).then_inc(merged, 1)
                    held(pool, merged, count + 3)

                FST = 6

                def finish(ic, ib, count):
                    rb = rden[:, :].rearrange("p (b h) -> p b h", h=H)[:, bass.ds(ib, 1), :]\
                        .rearrange("p a h -> p (a h)").unsqueeze(2).to_broadcast([P, H, F])
                    Ob = O[:, bass.ds(ib, 1), :, :].rearrange("p a h f -> p (a h) f")
                    rs = res[:, bass.ds(ib, 1), :].rearrange("p a f -> p (a f)")
                    xb = x1c[:, bass.ds(ib, 1), :].rearrange("p a f -> p (a f)")
                    t = tmp
                    seq = [lambda: nc.gpsimd.tensor_tensor(t[:, :, :], Ob, rb, ALU.mult),
                           lambda: nc.gpsimd.tensor_tensor(t[:, 0:4, :], t[:, 0:4, :], t[:, 4:8, :], ALU.add),
                           lambda: nc.gpsimd.tensor_tensor(t[:, 0:2, :], t[:, 0:2, :], t[:, 2:4, :], ALU.add),
                           lambda: nc.gpsimd.tensor_tensor(t[:, 0, :], t[:, 0, :], t[:, 1, :], ALU.add),
                           lambda: nc.gpsimd.tensor_tensor(t[:, 0, :], t[:, 0, :], pb[:, :], ALU.add),
                           lambda: nc.gpsimd.tensor_tensor(rs, t[:, 0, :], xb, ALU.add)]
                    for m, f in enumerate(seq):
                        f().then_inc(fstep, 1)
                        held(pool, fstep, count + m + 1)

                def store(ic):
                    pool.dma_start(out_v[:, bass.ds(ic * IB, IB), :], res[:, :, :]).then_inc(out_st, 16)

                def shifts(ic):
                    pool.dma_start(shift[:, :, :].rearrange("p b k -> p (b k)"), shift_dram[bass.ds(ic * P, P), :])\
                        .then_inc(shift_ld, 16)

                def step(S, half, ic, c, first, par, early):
                    pc = (c - 1) % n
                    pic = ic if c > 0 else ic - 1
                    last_class = pc == n - 1 and not first
                    for q in range(4):
                        for u in range(2):
                            stage(S, c, q, u, first and q == 0)
                        if c == 1 and not early:
                            if q == 0:
                                held(pool, rden_ok, ic)
                                held(pool, x1_ld, ic * 16)
                            finish(ic - 1, q, (ic - 1) * (FST * IB) + q * FST)
                            if q == 3:
                                store(ic - 1)
                    if last_class:
                        pool.dma_start(x1c[:, :, :].rearrange("p b f -> p (b f)"), x1_dram[bass.ds(pic * P, P), :])\
                            .then_inc(x1_ld, 16)
                    if not first:
                        scales(S, pic, pc)
                    if c == 0:
                        shifts(ic)
                    with pool.Fori(4, 12) as q:
                        stage(S, c, q, 0)
                        stage(S, c, q, 1)
                        if not first:
                            merge(S, pc, q - 4, (S - 1) * PER + (q - 4) * 3)
                    with pool.Fori(12, NT // 2) as q:
                        stage(S, c, q, 0)
                        stage(S, c, q, 1)
                    if c == 1 and not early:
                        held(pool, out_st, ic * 16)

                def tail(S, ic):
                    pool.dma_start(x1c[:, :, :].rearrange("p b f -> p (b f)"), x1_dram[ic * P:(ic + 1) * P, :])\
                        .then_inc(x1_ld, 16)
                    scales(S, ic, n - 1)
                    with pool.Fori(0, 2 * IB) as q:
                        merge(S, n - 1, q, (S - 1) * PER + q * 3)
                    pool.wait_ge(rden_ok, NI)
                    pool.wait_ge(x1_ld, NI * 16)
                    with pool.Fori(0, IB) as q:
                        finish(ic, q, ic * (FST * IB) + q * FST)
                    store(ic)
                    pool.wait_ge(out_st, NI * 16)

                class_steps(pool, kvals, step, tail)
            both_paths(pool, "Pool", program)

        @block.scalar
        def _(act):
            link = Chain(act, astep)
            for dst, w, bvec in ((qw, Qw, Qb), (kw, Kw, Kb), (vw, Vw, Vb)):
                act.dma_start(dst[0:F, :], w).then_inc(ld_l1, 16)
                act.dma_start(dst[F:F + 1, :], bvec.unsqueeze(0)).then_inc(ld_l1, 16)
            for k in range(KC):
                act.dma_start(av[:, :, k, :], a1[k].rearrange("(c p) h -> p c h", p=P)).then_inc(ld_l1, 16)
            act.dma_start(pw[:, :, :], Pw.rearrange("(h d) f -> d h f", d=F)).then_inc(ld_l1, 16)
            act.dma_start(pb[:, :], Pb.partition_broadcast(P)).then_inc(ld_l1, 16)
            act.wait_ge(ln_var, 1)
            nc.scalar.activation(stat[:, 4, :], stat[:, 2, :], ACT.Sqrt).then_inc(ln_std, 1)
            act.wait_ge(dshift, 1)
            nc.scalar.activation(th0[:, :], d0[:, :], ACT.Exp, scale=1.0 - SLOPE).then_inc(dexp, 1)
            nc.scalar.activation(W0e[:, :, F], d0[:, :], ACT.Exp, scale=SLOPE).then_inc(dexp, 1)
            for g in range(NI):
                act.wait_ge(rrow_z, g + 1)
                nc.scalar.activation(r0[:, g * CH:(g + 1) * CH], r0[:, g * CH:(g + 1) * CH], ACT.Exp,
                                     scale=-(1.0 - SLOPE)).then_inc(rrow_done, 1)

            def cast(ic, b):
                m = ic * IB + b
                act.wait_ge(raw_ld[b], (ic + 1) * 16)
                act.wait_ge(blk_done, m + 1)
                nc.scalar.activation(abf[:, b % 2, :], raw[:, b, :], ACT.Copy).then_inc(cast_done, 1)

            def positive(ic, b):
                act.wait_ge(ev_done, (ic * IB + b + 1) * NG)
                nc.scalar.activation(pos0[:, :, b * P:(b + 1) * P], code0[:, :, b * P:(b + 1) * P], ACT.Relu)\
                    .then_inc(pos_done, 1)

            act.sem_inc(cast_done, IB)
            with act.Fori(0, NI) as ic:
                cast(ic, 0)
                cast(ic, 1)
                act.wait_ge(t0_made, ic * NT + 1)
                for b in range(IB):
                    positive(ic, b)
                    if b + 2 < IB:
                        cast(ic, b + 2)
            act.wait_ge(elu_in, 1)
            nc.scalar.activation(sq1[:, :, :], sq1[:, :, :], ACT.Exp).then_inc(elu_exp, 1)
            act.wait_ge(ln_var, 2)
            nc.scalar.activation(stat[:, 4, :], stat[:, 2, :], ACT.Sqrt).then_inc(ln_std, 1)
            for g in range(NI):
                act.wait_ge(aT_z, g + 1)
                nc.scalar.activation(rT[:, g * CH:(g + 1) * CH], rT[:, g * CH:(g + 1) * CH], ACT.Exp,
                                     scale=-(1.0 - SLOPE)).then_inc(rT_done, 1)
            act.wait_ge(tab_in, 1)
            nc.scalar.activation(th[:, :, :], bt[:, :, :], ACT.Exp, scale=1.0 - SLOPE).then_inc(tab_exp, 1)
            nc.scalar.activation(dd[:, :, :], bt[:, :, :], ACT.Exp, scale=SLOPE).then_inc(tab_exp, 1)
            act.wait_ge(x1_st, 16)
            for t in range(NT):
                act.wait_ge(vp_ps, t + 1)
                nc.scalar.activation(vp[:, t, :], ps[:, 4 + t % 4, :], ACT.Copy).then_inc(vp_sb, 1)
            act.wait_ge(vp_sb, NT)
            act.wait_ge(tab_exp, 2)
            act.sem_inc(pre_end, 1)
            act.wait_ge(pre_end, 5)

            def program(kvals):
                n = len(kvals)

                def mask(S, c, q, u, early=False):
                    jt = q * 2 + u
                    num = S * NT + jt
                    if not early:
                        act.wait_ge(mask_made, num - 1)
                        held(act, t_made, (num - 1) * NQ)
                    nc.scalar.activation(Mt[:, u, :], code[:, bass.ds(jt, 1), :].rearrange("p a i -> p (a i)"),
                                         ACT.Abs, bias=classneg[:, c:c + 1]).then_inc(abs_done, 1)
                    act.wait_ge(abs_done, num + 1)
                    nc.scalar.activation(M[:, u, :], Mt[:, u, :], ACT.Relu, bias=onesF[:, 0:1], scale=-1.0)\
                        .then_inc(mask_made, 1)

                def factors(ic, c):
                    act.wait_ge(ab_arg, ic * (n - 1) + c)
                    nc.scalar.activation(ab[:, :, :], abarg[:, :, :], ACT.Exp).then_inc(ab_done, 1)

                def transposed_sums(S, b):
                    act.wait_ge(acc_tr, S * 6 + b + 1)
                    tr = ps[:, 6 + b % 2, :].rearrange("p (b c) -> p b c", b=IB)
                    if b % 3 < 2:
                        pair = (b // 3) * 2 + b % 3
                        dst, src = accT[:, :, 2 * pair:2 * pair + 2, :], tr.rearrange("p b (h f) -> p b h f", f=F)
                    else:
                        Q = b // 3
                        dst, src = denT[:, :, Q * 4:Q * 4 + 4], tr.rearrange("p b (h r) -> p b h r", r=32)[:, :, :, 0]
                    nc.scalar.activation(dst, src, ACT.Copy).then_inc(accT_done, 1)

                def evacuate(S, begin=False):
                    act.wait_ge(pe_quad, (S + 1) * (NT * NQ))
                    for b in range(6):
                        if not begin:
                            act.wait_ge(acc_tr, (S - 1) * 6 + b + 1)
                        nc.scalar.activation(accS[:, b, :], ps[:, b, :], ACT.Copy).then_inc(acc_ev, 1)

                def step(S, half, ic, c, first, par, early):
                    if c == 0:
                        held(act, code_ld[0], (ic + 1) * 16)
                    pc = (c - 1) % n
                    for q in range(4):
                        mask(S, c, q, 0, first and q == 0)
                        mask(S, c, q, 1, first and q == 0)
                        if q == 0 and not first:
                            evacuate(S - 1, early)
                        if not first and q > 0:
                            if q == 1 and not early:
                                act.wait_ge(merged, (S - 1) * (3 * 2 * IB))
                            transposed_sums(S - 1, 2 * q - 2)
                            transposed_sums(S - 1, 2 * q - 1)
                    if not first and pc > 0:
                        factors(ic if c > 0 else ic - 1, pc)
                    with act.Fori(2, NT // 8) as q2:
                        for e in range(2):
                            mask(S, c, q2 * 2 + e, 0)
                            mask(S, c, q2 * 2 + e, 1)
                    if c == 0:
                        held(act, code_ld[1], (ic + 1) * 16)
                    with act.Fori(NT // 8, NT // 4) as q2:
                        for e in range(2):
                            mask(S, c, q2 * 2 + e, 0)
                            mask(S, c, q2 * 2 + e, 1)

                def tail(S, ic):
                    evacuate(S - 1)
                    act.wait_ge(merged, (S - 1) * (3 * 2 * IB))
                    for b in range(6):
                        transposed_sums(S - 1, b)
                    factors(ic, n - 1)

                class_steps(act, kvals, step, tail)
            both_paths(act, "Activation", program)

        @block.vector
        def _(dve):
            link = Chain(dve, vstep)
            dve.wait_ge(ld_x, 16)
            layernorm(dve, link, xs[:, :, :], h0[:, :, :], sq0, 1)
            dve.wait_ge(w0T_ps, 1)
            nc.vector.tensor_copy(w0T[:, :], ps[0:F, 4, 0:F]).then_inc(w0T_sb, 1)
            dve.wait_ge(wa_ps, 1)
            nc.vector.tensor_copy(w0s[:, F:F + 2], ps[0:F, 5, 0:2]).then_inc(wa_sb, 1)
            nc.vector.tensor_copy(wrep[:, :], ps[0:F, 5, 0:1].to_broadcast([F, P])).then_inc(wa_sb, 1)
            for g in range(NI):
                dve.wait_ge(hT_ps, g + 1)
                nc.vector.tensor_copy(h0T[:, g * CH:(g + 1) * CH], ps[0:F, g % 4, :]).then_inc(hT_sb, 1)
            for g in range(NI):
                dve.wait_ge(wh_ps, g + 1)
                nc.vector.tensor_copy(wh[:, g * IB:(g + 1) * IB, :],
                                      ps[:, 4 + g % 4, 0:IB * (F + 2)].rearrange("p (t f) -> p t f", f=F + 2))\
                    .then_inc(wh_sb, 1)
            dve.wait_ge(wh_sb, NI)
            nc.vector.tensor_reduce(dm[:, 0:1], wh[:, :, F + 1], AX.X, ALU.max).then_inc(dmax_in, 1)
            nc.vector.tensor_reduce(whsum[:, :], wh[:, :, 0:F].rearrange("p t f -> p f t"), AX.X, ALU.add)\
                .then_inc(mean_in, 1)
            dve.wait_ge(dmax_out, 1)
            nc.vector.tensor_scalar(d0[:, :], wh[:, :, F + 1], dm[:, 1:2], None, ALU.subtract).then_inc(dshift, 1)
            for g in range(NI):
                dve.wait_ge(rrow_ps, g + 1)
                nc.vector.tensor_scalar(r0[:, g * CH:(g + 1) * CH], ps[:, g % 4, :], dm[:, 1:2], 0.0, ALU.add,
                                        ALU.max).then_inc(rrow_z, 1)
            dve.wait_ge(dexp, 2)
            nc.vector.tensor_tensor(W0e[:, :, 0:F], wh[:, :, 0:F], W0e[:, :, F:F + 1].to_broadcast([P, NT, F]),
                                    ALU.mult).then_inc(w0_ready, 1)
            dve.wait_ge(mean_ps, 1)
            nc.vector.tensor_copy(whmean[:, :], ps[:, 7, 0:F]).then_inc(mean_sb, 1)
            dve.wait_ge(rrow_done, NI)
            dve.wait_ge(mean_sb, 1)
            vbase = link.n
            FIN = 9
            dve.sem_inc(t0_made, 1)
            with dve.Fori(0, NI) as ic:
                for b in range(IB):
                    for g in range(NG):
                        m = (ic * IB + b) * NG + g
                        dve.wait_ge(tg_done, m + 1)
                        src = ps[:, g, :].bitcast(bf16).rearrange("p (t i) -> p t i", i=P)
                        nc.vector.tensor_scalar(code0[:, g * G8:(g + 1) * G8, b * P:(b + 1) * P], src, float(KC - 1),
                                                -1.0, ALU.min, ALU.max).then_inc(ev_done, 1)
                dve.wait_ge(pos_done, (ic + 1) * IB)
                for jt in range(NT):
                    if jt >= 4:
                        dve.wait_ge(t0_used, ic * NT + jt - 2)
                    else:
                        dve.wait_ge(t0_used, ic * NT + 1)
                    nc.vector.scalar_tensor_tensor(out=T0[:, jt % 4, :], in0=r0[:, bass.ds(ic * CH, CH)],
                                                   scalar=th0[:, jt:jt + 1], in1=pos0[:, jt, :], op0=ALU.max,
                                                   op1=ALU.min).then_inc(t0_made, 1)
                dve.wait_ge(t0_used, (ic + 1) * NT + 1)
                dve.wait_ge(code_st, (ic + 1) * 16)
                nc.vector.tensor_copy(A0s[:, :], ps[0:F + 1, 5, :]).then_inc(a0_sb, 1)
                dve.wait_ge(a0_tr, ic + 1)
                at = ps[:, 6, 0:IB * (F + 1)].rearrange("p (b f) -> p b f", f=F + 1)
                dn, pres, absent, rec = (den0[:, m, :] for m in range(4))

                def wide(a):
                    return a.unsqueeze(2).to_broadcast([P, IB, F])
                hv = h0[:, bass.ds(ic * IB, IB), :]
                mean_b = whmean[:, :].unsqueeze(1).to_broadcast([P, IB, F])
                seq = [lambda: nc.vector.tensor_copy(dn, at[:, :, F]),
                       lambda: nc.vector.tensor_scalar(pres, dn, 0.0, None, ALU.is_gt),
                       lambda: nc.vector.tensor_scalar(absent, pres, -1.0, 1.0, ALU.mult, ALU.add),
                       lambda: nc.vector.tensor_tensor(dn, dn, absent, ALU.add),
                       lambda: nc.vector.reciprocal(rec, dn),
                       lambda: nc.vector.tensor_tensor(rec, rec, pres, ALU.mult),
                       lambda: nc.vector.tensor_tensor(fin0[:, 0, :, :], at[:, :, 0:F], wide(rec), ALU.mult),
                       lambda: nc.vector.tensor_tensor(fin0[:, 1, :, :], mean_b, wide(absent), ALU.mult),
                       lambda: nc.vector.tensor_tensor(hv, fin0[:, 0, :, :], fin0[:, 1, :, :], ALU.add)]
                assert len(seq) == FIN
                for m, f in enumerate(seq):
                    f().then_inc(a0_fin, 1)
                    dve.wait_ge(a0_fin, ic * FIN + m + 1)
            dve.wait_ge(code_st, NI * 16)
            dve.wait_ge(flag_ps, 1)
            link(nc.vector.tensor_tensor(flagscr[:, :], ps[:, 4, 0:P], identF[:, :], ALU.mult))
            link(nc.vector.tensor_reduce(flagcol[:, 0:1], flagscr[:, :], AX.X, ALU.add))
            link(nc.vector.tensor_copy(flagcol[:, 1:2], ps[:, 4, P:P + 1]))
            nc.vector.tensor_tensor(flagcol[:, 2:3], flagcol[:, 0:1], flagcol[:, 1:2], ALU.not_equal)\
                .then_inc(flag_sum, 1)
            dve.wait_ge(flag_tot, 1)
            nc.vector.tensor_copy(flagi[:, :], flagcol[:, 3:4]).then_inc(flag_done, 1)
            nc.vector.tensor_scalar(sq1[:, :, :], h0[:, :, :], 0.0, None, ALU.min).then_inc(elu_in, 1)
            link(nc.vector.scalar_tensor_tensor(out=xs[:, :, :], in0=h0[:, :, :], scalar=0.0, in1=xs[:, :, :],
                                                op0=ALU.max, op1=ALU.add))
            dve.wait_ge(elu_exp, 1)
            link(nc.vector.scalar_tensor_tensor(out=xs[:, :, :], in0=sq1[:, :, :], scalar=-1.0, in1=xs[:, :, :],
                                                op0=ALU.add, op1=ALU.add))
            layernorm(dve, link, xs[:, :, :], h1[:, :, :], sq1[:, :, :], 2)
            link(nc.vector.memset(hT[F:F + 1, :], 1.0))
            link(nc.vector.memset(sa[:, KHV:KH], 0.0))
            link(nc.vector.memset(sbm[:, KHV:KH], 0.0))
            dve.wait_ge(wT_ps, 3)
            for dst, bank in ((qT, 4), (kT, 5)):
                nc.vector.tensor_copy(dst[:, :, :], ps[:, bank, 0:DC * (F + 1)].rearrange("p (c f) -> p c f", f=F + 1))\
                    .then_inc(wT_sb, 1)
            for hh in range(2):
                nc.vector.tensor_copy(vT[:, 4 * hh:4 * hh + 4, :],
                                      ps[0:F, 6 + hh, 0:4 * (F + 1)].rearrange("p (h f) -> p h f", f=F + 1))\
                    .then_inc(wT_sb, 1)
            for g in range(NI):
                dve.wait_ge(hT_ps, NI + g + 1)
                nc.vector.tensor_copy(hT[0:F, g * CH:(g + 1) * CH], ps[0:F, g % 4, :]).then_inc(hT_sb, 1)
            dve.wait_ge(s_ps, 1)
            nc.vector.tensor_copy(sa[:, 0:KHV], ps[0:F + 1, 4, 0:KHV]).then_inc(s_sb, 1)
            nc.vector.tensor_copy(sbm[:, 0:KHV], ps[0:F + 1, 5, 0:KHV]).then_inc(s_sb, 1)
            nc.vector.tensor_copy(vpw[:, :], ps[0:F + 1, 6, :]).then_inc(s_sb, 1)
            for g in range(NI):
                dve.wait_ge(bT_ps, g + 1)
                nc.vector.tensor_reduce(bm8[:, g:g + 1], ps[0:KH, g % 4, :], AX.X, ALU.max).then_inc(bT_red, 1)
            dve.wait_ge(bT_red, NI)
            link(nc.vector.tensor_reduce(bm8[:, NI:NI + 1], bm8[:, 0:NI], AX.X, ALU.max))
            nc.vector.tensor_copy(bmrep[:, :], bm8[:, NI:NI + 1].to_broadcast([KH, P])).then_inc(bmx_in, 1)
            dve.wait_ge(bmx_ps, 1)
            link(nc.vector.tensor_copy(bmx[:, :], ps[:, 7, 0:KH]))
            for g in range(NI):
                dve.wait_ge(aT_ps, g + 1)
                nc.vector.tensor_scalar(rT[:, g * CH:(g + 1) * CH], ps[0:KH, g % 4, :], bm8[:, NI:NI + 1], 0.0,
                                        ALU.add, ALU.max).then_inc(aT_z, 1)
            for g in range(2 * NI):
                dve.wait_ge(ab_ps, g + 1)
                t0 = (g % NI) * IB
                dst = (bt if g < NI else LL)[:, t0:t0 + IB, :]
                nc.vector.tensor_tensor(dst, ps[:, 4 + g % 3, 0:IB * KH].rearrange("p (t c) -> p t c", c=KH),
                                        bmx[:, :].unsqueeze(1).to_broadcast([P, IB, KH]),
                                        ALU.subtract if g < NI else ALU.add).then_inc(ab_sb, 1)
            dve.wait_ge(ab_sb, 2 * NI)
            nc.vector.tensor_scalar(bt[:, :, :], bt[:, :, :], 0.0, None, ALU.min).then_inc(tab_in, 1)
            nc.vector.scalar_tensor_tensor(out=LL[:, :, :], in0=LL[:, :, :], scalar=SLOPE, in1=LL[:, :, :],
                                           op0=ALU.mult, op1=ALU.max).then_inc(shift_ok, 1)
            dve.wait_ge(shift_ok, 1)
            dve.wait_ge(tab_in, 1)
            dve.sem_inc(pre_end, 1)
            dve.wait_ge(pre_end, 5)

            def program(kvals):
                n = len(kvals)

                def probs(S, c, par, q, u, early=False):
                    jt = q * 2 + u
                    num = S * NT + jt
                    dve.wait_ge(mask_made, num + 1)
                    for h in range(H):
                        if h % 4 == 0 and not early:
                            dve.wait_ge(pe_quad, (num - 2) * NQ + h // 4 + 1)
                        last = nc.vector.scalar_tensor_tensor(
                            out=T[:, u, h, :], in0=R[:, par, h, :],
                            scalar=th[:, bass.ds(jt, 1), c * H + h:c * H + h + 1].rearrange("p a b -> p (a b)"),
                            in1=M[:, u, :], op0=ALU.max, op1=ALU.mult)
                        if h % 4 == 3:
                            last.then_inc(t_made, 1)

                def recip(S, ic):
                    dve.wait_ge(den_fin, ic + 1)
                    nc.vector.reciprocal(rden[:, :], den[:, :]).then_inc(rden_ok, 1)

                def step(S, half, ic, c, first, par, early):
                    dve.wait_ge(r_ld[par], (half + 1) * 16)
                    probs(S, c, par, 0, 0, first)
                    probs(S, c, par, 0, 1, first)
                    probs(S, c, par, 1, 0)
                    probs(S, c, par, 1, 1)
                    with dve.Fori(1, NT // 4) as q2:
                        for e in range(2):
                            probs(S, c, par, q2 * 2 + e, 0)
                            probs(S, c, par, q2 * 2 + e, 1)
                    if c == 0 and not first:
                        recip(S, ic - 1)

                class_steps(dve, kvals, step, lambda S, ic: recip(S, ic))
            both_paths(dve, "DVE", program)

        @block.tensor
        def _(pe):
            pe.wait_ge(consts, 6 + CL)
            pe.wait_ge(ld_w0, 48)
            nc.tensor.transpose(ps[0:F, 4, 0:F], w0s[:, 0:F], identF[0:F, 0:F]).then_inc(w0T_ps, 1)
            pe.wait_ge(w0T_sb, 1)
            nc.tensor.matmul(ps[0:F, 5, 0:2], w0T[:, :], a0s[:, :], start=True, stop=True).then_inc(wa_ps, 1)

            def transposed(src, done, base):
                for g in range(NI):
                    if base + g >= 4:
                        pe.wait_ge(hT_sb, base + g - 3)
                    for b in range(IB):
                        last = nc.tensor.transpose(ps[0:F, g % 4, b * P:(b + 1) * P], src[:, g * IB + b, :],
                                                   identF[:, :])
                    last.then_inc(hT_ps, 1)
            pe.wait_ge(ln_done, 1)
            transposed(h0, ln_done, 0)
            pe.wait_ge(wa_sb, 2)
            for g in range(NI):
                pe.wait_ge(hT_sb, g + 1)
                if g >= 4:
                    pe.wait_ge(wh_sb, g - 3)
                for b in range(IB):
                    t = g * IB + b
                    last = nc.tensor.matmul(ps[:, 4 + g % 4, b * (F + 2):(b + 1) * (F + 2)],
                                            h0T[:, t * P:(t + 1) * P], w0s[:, :], start=True, stop=True)
                last.then_inc(wh_ps, 1)
            for g in range(NI):
                if g >= 4:
                    pe.wait_ge(rrow_z, g - 3)
                nc.tensor.matmul(ps[:, g % 4, :], wrep[:, :], h0T[:, g * CH:(g + 1) * CH], start=True, stop=True)\
                    .then_inc(rrow_ps, 1)
            pe.wait_ge(mean_in, 1)
            pe.wait_ge(wh_sb, NI)
            nc.tensor.matmul(ps[:, 7, 0:F], meanmat[:, :], whsum[:, :], start=True, stop=True).then_inc(mean_ps, 1)
            pe.wait_ge(w0_ready, 1)
            pe.wait_ge(rrow_z, NI)
            nc.tensor.matmul(ps[:, 4, 0:P + 1], zerosB[:, 0:P], zerosB[:, :], start=True, stop=False,
                             skip_group_check=True)
            pe.sem_inc(blk_done, 2)
            pe.sem_inc(t0_used, 1)
            with pe.Fori(0, NI) as ic:
                for b in range(IB):
                    pe.wait_ge(cast_done, (ic + 1) * IB + b + 1)
                    for g in range(NG):
                        if b > 0:
                            pe.wait_ge(ev_done, (ic * IB + b - 1) * NG + g + 1)
                        for e in range(G8):
                            j = (g * G8 + e) * P
                            blk = abf[:, b % 2, j:j + P]
                            dst = ps[:, g, :].bitcast(bf16)[:, e * P:(e + 1) * P]
                            last = nc.tensor.transpose(dst, blk, identB[:, :])
                            nc.tensor.matmul(ps[:, 4, 0:P], blk, blk, start=False, stop=False, skip_group_check=True)
                            summed = nc.tensor.matmul(ps[:, 4, P:P + 1], blk, onesB[:, :], start=False, stop=False,
                                                      skip_group_check=True)
                        last.then_inc(tg_done, 1)
                    summed.then_inc(blk_done, 1)
                for jt in range(NT):
                    pe.wait_ge(t0_made, ic * NT + jt + 2)
                    nc.tensor.matmul(ps[0:F + 1, 5, :], W0e[:, jt, :], T0[:, jt % 4, :], start=(jt == 0),
                                     stop=(jt == NT - 1)).then_inc(t0_used, 1)
                pe.wait_ge(a0_sb, ic + 1)
                for b in range(IB):
                    last = nc.tensor.transpose(ps[:, 6, b * (F + 1):(b + 1) * (F + 1)], A0s[:, b * P:(b + 1) * P],
                                               identF[0:F + 1, 0:F + 1])
                last.then_inc(a0_tr, 1)
            nc.tensor.matmul(ps[:, 4, 0:P + 1], zerosB[:, 0:P], zerosB[:, :], start=False, stop=True,
                             skip_group_check=True).then_inc(flag_ps, 1)
            pe.wait_ge(ld_l1, 16 * (6 + KC + 2))
            pe.wait_ge(flag_sum, 1)
            pe.wait_ge(a0_fin, NI * 9)
            for w, bank in ((qw, 4), (kw, 5)):
                for c in range(DC):
                    last = nc.tensor.transpose(ps[:, bank, c * (F + 1):(c + 1) * (F + 1)], w[:, c * P:(c + 1) * P],
                                               identF[0:F + 1, 0:F + 1])
                last.then_inc(wT_ps, 1)
            for h in range(H):
                last = nc.tensor.transpose(ps[0:F, 6 + h // 4, (h % 4) * (F + 1):(h % 4 + 1) * (F + 1)],
                                           vw[:, h * F:(h + 1) * F], identF[0:F + 1, 0:F + 1])
            last.then_inc(wT_ps, 1)
            pe.wait_ge(wT_sb, 4)
            for w, bank, half in ((qT, 4, 0), (kT, 5, 1)):
                for c in range(DC):
                    nc.tensor.matmul(ps[0:F + 1, bank, 0:KHV], w[:, c, :],
                                     av[:, half * DC + c, :, :].rearrange("p k h -> p (k h)"), start=(c == 0),
                                     stop=(c == DC - 1))
            for h in range(H):
                last = nc.tensor.matmul(ps[0:F + 1, 6, h * F:(h + 1) * F], vT[:, h, :], pw[:, h, :], start=True,
                                        stop=True)
            last.then_inc(s_ps, 1)
            pe.wait_ge(ln_done, 2)
            transposed(h1, ln_done, NI)
            pe.wait_ge(hT_sb, 2 * NI)
            pe.wait_ge(s_sb, 3)
            for g in range(NI):
                if g >= 4:
                    pe.wait_ge(bT_red, g - 3)
                nc.tensor.matmul(ps[0:KH, g % 4, :], sbm[:, :], hT[:, g * CH:(g + 1) * CH], start=True, stop=True)\
                    .then_inc(bT_ps, 1)
            pe.wait_ge(bmx_in, 1)
            nc.tensor.matmul(ps[:, 7, 0:KH], bmrep[:, :], identF[0:KH, 0:KH], start=True, stop=True).then_inc(bmx_ps, 1)
            for g in range(NI):
                if g >= 4:
                    pe.wait_ge(aT_z, g - 3)
                nc.tensor.matmul(ps[0:KH, g % 4, :], sa[:, :], hT[:, g * CH:(g + 1) * CH], start=True, stop=True)\
                    .then_inc(aT_ps, 1)
            for g in range(2 * NI):
                if g >= 3:
                    pe.wait_ge(ab_sb, g - 2)
                for b in range(IB):
                    t = (g % NI) * IB + b
                    last = nc.tensor.matmul(ps[:, 4 + g % 3, b * KH:(b + 1) * KH], hT[:, t * P:(t + 1) * P],
                                            (sbm if g < NI else sa)[:, :], start=True, stop=True)
                last.then_inc(ab_ps, 1)
            pe.wait_ge(ab_sb, 2 * NI)
            for t in range(NT):
                if t >= 4:
                    pe.wait_ge(vp_sb, t - 3)
                nc.tensor.matmul(ps[:, 4 + t % 4, :], hT[:, t * P:(t + 1) * P], vpw[:, :], start=True, stop=True)\
                    .then_inc(vp_ps, 1)
            pe.wait_ge(vp_sb, NT)
            pe.wait_ge(aT_z, NI)
            pe.wait_ge(rT_st, 16)
            pe.sem_inc(pre_end, 2)
            pe.wait_ge(pre_end, 5)

            def program(kvals):
                n = len(kvals)

                def products(S, q, u, begin, end, first=False):
                    jt = q * 2 + u
                    num = S * NT + jt
                    pe.wait_ge(w_staged, (num + 1) * 2)
                    for Q in range(NQ):
                        pe.wait_ge(t_made, num * NQ + Q + 1)
                        if begin and not first:
                            pe.wait_ge(acc_ev, (S - 1) * 6 + 3 * Q + 3)
                        for hh in range(4):
                            h = 4 * Q + hh
                            p0 = F * (hh % 2)
                            nc.tensor.matmul(ps[p0:p0 + F, 3 * Q + hh // 2, :], Ws[:, u, h, :], T[:, u, h, :],
                                             start=begin, stop=end)
                        for hh in range(4):
                            h = 4 * Q + hh
                            last = nc.tensor.matmul(ps[32 * hh:32 * hh + 32, 3 * Q + 2, :], Ds[:, u, h, :], T[:, u, h, :],
                                                    start=begin, stop=end, tile_position=(0, 32 * hh))
                        last.then_inc(pe_quad, 1)

                def transposed_sums(S, b, skip=False):
                    pe.wait_ge(acc_ev, S * 6 + b + 1)
                    if not skip:
                        pe.wait_ge(accT_done, S * 6 + b - 1)
                    for i in range(IB):
                        last = nc.tensor.transpose(ps[:, 6 + b % 2, i * P:(i + 1) * P],
                                                   accS[:, b, i * P:(i + 1) * P], identF[:, :])
                    last.then_inc(acc_tr, 1)

                def step(S, half, ic, c, first, par, early):
                    for q in range(3):
                        products(S, q, 0, q == 0, False, first)
                        products(S, q, 1, False, False)
                        if not first:
                            for b in (2 * q, 2 * q + 1):
                                transposed_sums(S - 1, b, early and b < 2)
                    products(S, 3, 0, False, False)
                    products(S, 3, 1, False, False)
                    with pe.Fori(2, NT // 4 - 1) as q2:
                        for e in range(2):
                            products(S, q2 * 2 + e, 0, False, False)
                            products(S, q2 * 2 + e, 1, False, False)
                    products(S, NT // 2 - 2, 0, False, False)
                    products(S, NT // 2 - 2, 1, False, False)
                    products(S, NT // 2 - 1, 0, False, False)
                    products(S, NT // 2 - 1, 1, False, True)

                def tail(S, ic):
                    for b in range(6):
                        transposed_sums(S - 1, b)

                class_steps(pe, kvals, step, tail)
            both_paths(pe, "PE", program)


_INS = ['x', 'adj', 'L0_gnn_W', 'L0_gnn_a', 'L1_gnn_Qw', 'L1_gnn_Qb', 'L1_gnn_Kw', 'L1_gnn_Kb', 'L1_gnn_Vw',
        'L1_gnn_Vb', 'L1_gnn_a', 'L1_gnn_Pw', 'L1_gnn_Pb']


def kernel(**inputs):
    import numpy as _np
    import concourse.bacc as _bacc
    from concourse import mybir as _mybir
    from concourse.bass_utils import run_bass_kernel_spmd as _run

    nc = _bacc.Bacc("TRN2", target_bir_lowering=False, num_devices=1)
    arrays, args = {}, []
    for name in _INS:
        a = _np.ascontiguousarray(inputs[name])
        arrays[f"in_{name}"] = a
        args.append(nc.dram_tensor(f"in_{name}", a.shape, _mybir.dt.from_np(a.dtype), kind="ExternalInput").ap())
    shape = arrays["in_x"].shape
    out = nc.dram_tensor("out_0", shape, _mybir.dt.float32, kind="ExternalOutput").ap()
    two_layer_graph_attention(nc, *args, out)
    r = _run(nc, [arrays], core_ids=[0])
    return r.results[0]["out_0"]
```

```python
from contextlib import ExitStack

import concourse.bass as bass
from concourse import mybir


def two_layer_graph_attention(nc, x, adj, W0, a0, Qw, Qb, Kw, Kb, Vw, Vb, a1, Pw, Pb, out):
    f32 = mybir.dt.float32
    bf16 = mybir.dt.bfloat16
    i8 = mybir.dt.int8
    i32 = mybir.dt.int32
    ALU = mybir.AluOpType
    ACT = mybir.ActivationFunctionType
    AX = mybir.AxisListType

    N, F = x.shape
    P = 128
    NT = N // P
    CH = 512
    NI = N // CH
    IB = CH // P
    KC, _, H = a1.shape
    HD = H * F
    CL = KC + 1
    KH = CL * H
    KHV = KC * H
    DC = HD // P
    NQ = H // 4
    G8 = 8
    NG = NT // G8
    GW = G8 * P
    TS = 8
    SLOPE = 0.2
    EPS = 1e-5
    ABSENT = 1e30

    x_v = x.rearrange("(t p) f -> p t f", p=P)
    out_v = out.rearrange("(t p) f -> p t f", p=P)
    adj_v = adj.rearrange("(m p) j -> m p j", p=P)
    code_dram = nc.dram_tensor("code_scratch", (NI * P, NT * CH), i8).ap()
    x1_dram = nc.dram_tensor("x1_scratch", (NI * P, IB * F), f32).ap()
    shift_dram = nc.dram_tensor("shift_scratch", (NI * P, IB * KH), f32).ap()
    r_dram = nc.dram_tensor("r_scratch", (KH, N), f32).ap()

    ctx = ExitStack()
    with ctx:
        def sem(name):
            return ctx.enter_context(nc.semaphore(name))

        def sb(scope, name, shape, dt):
            return scope.enter_context(nc.sbuf_tensor(name, shape, dt))

        identF = sb(ctx, "identF", [P, P], f32)
        onesF = sb(ctx, "onesF", [P, 1], f32)
        pb = sb(ctx, "pb", [P, F], f32)
        classneg = sb(ctx, "classneg", [P, CL], f32)
        flagi = sb(ctx, "flagi", [P, 1], i32)

        wsc = ExitStack()
        qw = sb(wsc, "qw", [F + 1, HD], f32)
        kw = sb(wsc, "kw", [F + 1, HD], f32)
        vw = sb(wsc, "vw", [F + 1, HD], f32)
        av = sb(wsc, "av", [P, 2 * DC, KC, H], f32)
        pw = sb(wsc, "pw", [F, H, F], f32)
        meanmat = sb(wsc, "meanmat", [P, P], f32)
        zerosB = sb(wsc, "zerosB", [P, CH], bf16)
        identB = sb(wsc, "identB", [P, P], bf16)
        onesB = sb(wsc, "onesB", [P, 1], bf16)
        stat = sb(wsc, "stat", [P, 5, NT], f32)
        flagcol = sb(wsc, "flagcol", [1, 2], f32)
        halfneg = sb(wsc, "halfneg", [P, 1], f32)
        xs = sb(wsc, "xs", [P, NT, F], f32)
        h0 = sb(wsc, "h0", [P, NT, F], f32)

        l0 = ExitStack()
        raw = sb(l0, "raw", [P, NG, IB, GW], i32)
        abf = sb(l0, "abf", [P, 2, IB, GW], bf16)
        code0 = sb(l0, "code0", [P, NT, CH], i8)
        pos0 = sb(l0, "pos0", [P, NT, CH], i8)
        sqc = sb(l0, "sqc", [P, G8, CH], bf16)
        r0 = sb(l0, "r0", [P, N], f32)
        share0 = sb(l0, "share0", [P, N], f32)
        sq0 = share0[:, 0:NT * F].rearrange("p (t f) -> p t f", f=F)
        h0T = share0[0:F, :]
        T0 = share0[:, 0:TS * CH].rearrange("p (s i) -> p s i", i=CH)
        wh = sb(l0, "wh", [P, NT, F + 2], f32)
        w0s = sb(l0, "w0s", [F, F + 2], f32)
        w0T = sb(l0, "w0T", [F, F], f32)
        a0s = sb(l0, "a0s", [F, 2], f32)
        wrep = sb(l0, "wrep", [F, P], f32)
        W0e = wh[:, :, 0:F]
        W0d = sb(l0, "W0d", [P, NT, 32], f32)
        pairI = sb(l0, "pairI", [P, F], f32)
        sel = sb(l0, "sel", [P, 1], f32)
        th0 = sb(l0, "th0", [P, NT], f32)
        d0 = sb(l0, "d0", [P, NT], f32)
        dm = sb(l0, "dm", [P, 4], f32)
        whsum = sb(l0, "whsum", [P, F], f32)
        whmean = sb(l0, "whmean", [P, F], f32)
        A0s = sb(l0, "A0s", [P, 2, CH], f32)
        fin0 = sb(l0, "fin0", [P, 2, IB, F], f32)
        den0 = sb(l0, "den0", [P, 4, IB], f32)
        l0.close()
        wsc.close()

        l1 = ExitStack()
        vp = sb(l1, "vp", [P, NT, HD], f32)
        th = sb(l1, "th", [P, NT, KH], f32)
        dd = sb(l1, "dd", [P, NT, KH], f32)
        code = sb(l1, "code", [P, NT, CH], i8)
        pre = ExitStack()
        LL = sb(pre, "LL", [P, NT, KH], f32)
        hT = sb(pre, "hT", [F + 1, N], f32)
        rT = sb(pre, "rT", [KH, N], f32)
        h1 = sb(pre, "h1", [P, NT, F], f32)
        sq1 = sb(pre, "sq1", [P, NT, F], f32)
        bt = sb(pre, "bt", [P, NT, KH], f32)
        qT = sb(pre, "qT", [P, DC, F + 1], f32)
        kT = sb(pre, "kT", [P, DC, F + 1], f32)
        vT = sb(pre, "vT", [F, H, F + 1], f32)
        sa = sb(pre, "sa", [F + 1, KH], f32)
        sbm = sb(pre, "sbm", [F + 1, KH], f32)
        vpw = sb(pre, "vpw", [F + 1, HD], f32)
        bm8 = sb(pre, "bm8", [KH, NI + 1], f32)
        bmrep = sb(pre, "bmrep", [KH, P], f32)
        bmx = sb(pre, "bmx", [P, KH], f32)
        pre.close()
        R = sb(l1, "R", [P, 2, H, CH], f32)
        T = sb(l1, "T", [P, 2, H, CH], f32)
        x1c = sb(l1, "x1c", [P, IB, F], f32)
        shift = sb(l1, "shift", [P, IB, KH], f32)
        Ws = sb(l1, "Ws", [P, 2, H, F], f32)
        Ds = sb(l1, "Ds", [P, 2, H, 32], f32)
        Mt = sb(l1, "Mt", [P, 2, CH], bf16)
        M = sb(l1, "M", [P, 2, CH], bf16)
        accS = sb(l1, "accS", [P, 6, CH], f32)
        accT = sb(l1, "accT", [P, IB, H, F], f32)
        O = sb(l1, "O", [P, IB, H, F], f32)
        tmp = sb(l1, "tmp", [P, H, F], f32)
        denT = sb(l1, "denT", [P, IB, H], f32)
        tiny = sb(l1, "tiny", [P, 4, IB * H], f32)
        abarg = sb(l1, "abarg", [P, 2, IB * H], f32)
        ab = sb(l1, "ab", [P, 2, IB * H], f32)
        cst = sb(l1, "cst", [P, IB * H], f32)
        den = sb(l1, "den", [P, IB * H], f32)
        rden = sb(l1, "rden", [P, IB * H], f32)
        res = sb(l1, "res", [P, IB, F], f32)
        l1.close()

        ps = ctx.enter_context(nc.psum_tensor("ps", [P, 8, CH], f32))

        ld_x, ld_w0, ld_l1 = sem("ld_x"), sem("ld_w0"), sem("ld_l1")
        consts = sem("consts")
        vstep, astep, pstep = sem("vstep"), sem("astep"), sem("pstep")
        ln_var, ln_std, ln_done = sem("ln_var"), sem("ln_std"), sem("ln_done")
        hT_ps, hT_sb = sem("hT_ps"), sem("hT_sb")
        w0T_ps, w0T_sb, wa_ps, wa_sb = sem("w0T_ps"), sem("w0T_sb"), sem("wa_ps"), sem("wa_sb")
        wh_ps, wh_sb = sem("wh_ps"), sem("wh_sb")
        dmax_in, dmax_out, dshift, dexp = sem("dmax_in"), sem("dmax_out"), sem("dshift"), sem("dexp")
        rrow_ps, rrow_z, rrow_done = sem("rrow_ps"), sem("rrow_z"), sem("rrow_done")
        w0_ready, mean_in, mean_ps, mean_sb = sem("w0_ready"), sem("mean_in"), sem("mean_ps"), sem("mean_sb")
        raw_ld = [sem(f"raw_ld{g}") for g in range(NG)]
        cast_done, tg_done, ev_done = sem("cast_done"), sem("tg_done"), sem("ev_done")
        pos_done, code_st = sem("pos_done"), [sem(f"code_st{g}") for g in range(NG)]
        t0_made, t0_used = sem("t0_made"), sem("t0_used")
        a0_sb, a0_tr, a0_fin = sem("a0_sb"), sem("a0_tr"), sem("a0_fin")
        flag_ps, flag_sum, flag_done = sem("flag_ps"), sem("flag_sum"), sem("flag_done")
        sq_made, sq_used = sem("sq_made"), sem("sq_used")
        elu_in, elu_exp = sem("elu_in"), sem("elu_exp")
        wT_ps, wT_sb, s_ps, s_sb = sem("wT_ps"), sem("wT_sb"), sem("s_ps"), sem("s_sb")
        bT_ps, bT_red, bmx_in, bmx_ps = sem("bT_ps"), sem("bT_red"), sem("bmx_in"), sem("bmx_ps")
        ab_ps, ab_sb, aT_ps, aT_z, rT_done, rT_st = (sem("ab_ps"), sem("ab_sb"), sem("aT_ps"), sem("aT_z"),
                                                   sem("rT_done"), sem("rT_st"))
        tab_in, tab_exp, vp_ps, vp_sb = sem("tab_in"), sem("tab_exp"), sem("vp_ps"), sem("vp_sb")
        pre_end, x1_st, shift_ok, shift_st = sem("pre_end"), sem("x1_st"), sem("shift_ok"), sem("shift_st")
        x1_ld, shift_ld = sem("x1_ld"), sem("shift_ld")
        r_ld = [sem("r_ld0"), sem("r_ld1")]
        code_ld = [sem("code_ld0"), sem("code_ld1")]
        abs_done, mask_made, t_made, pe_quad = sem("abs_done"), sem("mask_made"), sem("t_made"), sem("pe_quad")
        w_staged, acc_ev, acc_tr, accT_done = sem("w_staged"), sem("acc_ev"), sem("acc_tr"), sem("accT_done")
        ab_arg, ab_done, merged, den_fin, rden_ok = (sem("ab_arg"), sem("ab_done"), sem("merged"), sem("den_fin"),
                                                    sem("rden_ok"))
        mstep, fstep = sem("mstep"), sem("fstep")
        out_st = sem("out_st")
        passed = sem("passed")

        class Chain:

            def __init__(self, eng, s):
                self.eng, self.s, self.n = eng, s, 0

            def __call__(self, ins):
                self.n += 1
                ins.then_inc(self.s, 1)
                self.eng.wait_ge(self.s, self.n)

        def held(eng, s, value):
            eng.wait_ge(s, value)
            eng.sem_inc(passed, 1)

        def layernorm(dve, link, src, cen, sq, which):
            s, mean, v, rr, t = (stat[:, n, :] for n in range(5))

            def wide(a):
                return a.unsqueeze(2).to_broadcast([P, NT, F])
            link(nc.vector.tensor_reduce(s, src, AX.X, ALU.add))
            link(nc.vector.tensor_scalar(mean, s, 1.0 / F, None, ALU.mult))
            link(nc.vector.tensor_tensor(cen, src, wide(mean), ALU.subtract))
            link(nc.vector.tensor_tensor(sq, cen, cen, ALU.mult))
            link(nc.vector.tensor_reduce(s, sq, AX.X, ALU.add))
            nc.vector.tensor_scalar(v, s, 1.0 / F, EPS, ALU.mult, ALU.add).then_inc(ln_var, 1)
            dve.wait_ge(ln_var, which)
            dve.wait_ge(ln_std, which)
            link(nc.vector.reciprocal(rr, t))
            link(nc.vector.tensor_tensor(t, rr, rr, ALU.mult))
            link(nc.vector.tensor_tensor(t, t, v, ALU.mult))
            link(nc.vector.tensor_scalar(t, t, -0.5, 1.5, ALU.mult, ALU.add))
            link(nc.vector.tensor_tensor(rr, rr, t, ALU.mult))
            nc.vector.scalar_tensor_tensor(out=cen, in0=cen, scalar=0.0, in1=wide(rr), op0=ALU.max,
                                           op1=ALU.mult).then_inc(ln_done, 1)
            dve.wait_ge(ln_done, which)

        def class_steps(eng, kvals, step, tail):
            n = len(kvals)
            u = 1 if n % 2 == 0 else 2

            def body(I, peeled):
                for e in range(u):
                    for c in range(n):
                        s = e * n + c
                        step(I * (u * n) + s, I * (u * n // 2) + s // 2, I * u + e, c, peeled and s == 0,
                             s % 2, peeled and s < 2)
            body(0, True)
            with eng.Fori(1, NI // u) as I:
                body(I, False)
            tail(NI * n, NI - 1)

        def both_paths(eng, engine_type, program):
            eng.wait_ge(flag_done, 1)
            flag = eng.value_load(flagi[0:1, 0:1], min_val=0, max_val=1)
            with eng.If(flag < 1):
                program([0, 1])
            with eng.Else():
                program(list(range(KC)) + [-1])

        block = ctx.enter_context(nc.Block())

        @block.sync
        def _(sp):
            sp.dma_start(xs[:, :, :], x_v).then_inc(ld_x, 16)
            sp.dma_start(w0s[:, 0:F], W0).then_inc(ld_w0, 16)
            for half in range(2):
                sp.dma_start(a0s[:, half:half + 1], a0[half * F:(half + 1) * F, :]).then_inc(ld_w0, 16)
            def load(ic, g):
                sp.dma_start(raw[:, g, :, :],
                             adj_v[bass.ds(ic * IB, IB), :, g * GW:(g + 1) * GW].rearrange("b p j -> p b j"))\
                    .then_inc(raw_ld[g], 16)
            for g in range(NG):
                load(0, g)
            with sp.Fori(1, NI) as ic:
                for g in range(NG):
                    sp.wait_ge(cast_done, (ic - 1) * NG + g + 1)
                    load(ic, g)
            sp.wait_ge(ln_done, 2)
            sp.dma_start(x1_dram.rearrange("(c p) f -> p c f", p=P),
                         xs[:, :, :].rearrange("p (c b) f -> p c (b f)", b=IB)).then_inc(x1_st, 16)
            sp.wait_ge(rT_done, NI)
            sp.dma_start(r_dram, rT[:, :]).then_inc(rT_st, 16)
            sp.wait_ge(shift_ok, 1)
            sp.dma_start(shift_dram.rearrange("(c p) f -> p c f", p=P),
                         LL[:, :, :].rearrange("p (c b) k -> p c (b k)", b=IB)).then_inc(shift_st, 16)
            sp.wait_ge(x1_st, 16)
            sp.wait_ge(rT_st, 16)
            sp.wait_ge(shift_st, 16)
            for g in range(NG):
                sp.wait_ge(code_st[g], 16 * NI)
            sp.wait_ge(cast_done, NI * NG)
            for hf in range(2):
                sp.dma_start(code[:, hf * NT // 2:(hf + 1) * NT // 2, :],
                             code_dram[0:P, hf * NT // 2 * CH:(hf + 1) * NT // 2 * CH]
                             .rearrange("p (t i) -> p t i", i=CH)).then_inc(code_ld[hf], 16)
            sp.sem_inc(pre_end, 1)
            sp.wait_ge(pre_end, 5)

            def program(kvals):
                n = len(kvals)

                def step(S, half, ic, c, first, par, early):
                    if not early:
                        sp.wait_ge(t_made, (S - 1) * (NT * NQ))
                    k = c
                    sp.dma_start(R[:, par, :, :],
                                 r_dram[k * H:(k + 1) * H, bass.ds(ic * CH, CH)].partition_broadcast(P))\
                        .then_inc(r_ld[par], 16)
                    if c == 0 and not first:
                        for hf in range(2):
                            held(sp, mask_made, S * NT - (1 - hf) * (NT // 2))
                            w = NT // 2
                            sp.dma_start(code[:, hf * w:(hf + 1) * w, :],
                                         code_dram[bass.ds(ic * P, P), hf * w * CH:(hf + 1) * w * CH]
                                         .rearrange("p (t i) -> p t i", t=w)).then_inc(code_ld[hf], 16)

                class_steps(sp, kvals, step, lambda S, ic: None)
            both_paths(sp, "SP", program)

        @block.gpsimd
        def _(pool):
            link = Chain(pool, pstep)
            link(nc.gpsimd.memset(identF[:, :], 0.0))
            link(nc.gpsimd.memset(identB[:, :], 0.0))
            for m in (identF, identB):
                nc.gpsimd.affine_select(out=m[:, :], in_=m[:, :], compare_op=ALU.not_equal, fill=1.0, base=0,
                                        pattern=[[-1, P]], channel_multiplier=1).then_inc(consts, 1)
            nc.gpsimd.memset(meanmat[:, :], 1.0 / N).then_inc(consts, 1)
            nc.gpsimd.memset(zerosB[:, :], 0.0).then_inc(consts, 1)
            nc.gpsimd.memset(onesB[:, :], 1.0).then_inc(consts, 1)
            nc.gpsimd.memset(halfneg[:, :], -0.5).then_inc(consts, 1)
            nc.gpsimd.memset(onesF[:, :], 1.0).then_inc(consts, 1)
            for c in range(CL):
                nc.gpsimd.memset(classneg[:, c:c + 1], float(-c if c < KC else 1)).then_inc(consts, 1)
            pool.wait_ge(dmax_in, 1)
            nc.gpsimd.partition_all_reduce(dm[:, 1:2], dm[:, 0:1], P, bass.bass_isa.ReduceOp.max)\
                .then_inc(dmax_out, 1)
            with pool.Fori(0, NI) as ic:
                for g in range(NG):
                    held(pool, ev_done, (ic * NG + g + 1) * IB)
                    pool.dma_start(code_dram[bass.ds(ic * P, P), g * G8 * CH:(g + 1) * G8 * CH],
                                   code0[:, g * G8:(g + 1) * G8, :].rearrange("p t i -> p (t i)")).then_inc(code_st[g], 16)
            pool.wait_ge(pre_end, 5)
            pbase = link.n

            def program(kvals):
                n = len(kvals)

                def stage(S, c, q, u, early=False):
                    jt = q * 2 + u
                    if not early:
                        held(pool, pe_quad, (S * NT + jt - 1) * NQ)
                    dj = dd[:, bass.ds(jt, 1), c * H:(c + 1) * H].rearrange("p a h -> p (a h)")
                    nc.gpsimd.tensor_tensor(Ws[:, u, :, :],
                                            vp[:, bass.ds(jt, 1), :].rearrange("p a (h f) -> p (a h) f", h=H),
                                            dj.unsqueeze(2).to_broadcast([P, H, F]), ALU.mult).then_inc(w_staged, 1)
                    nc.gpsimd.tensor_copy(Ds[:, u, :, :], dj.unsqueeze(2).to_broadcast([P, H, 32]))\
                        .then_inc(w_staged, 1)

                PER = 3 * 2 * IB
                CSTEPS = 20

                def scales(S, ic, c):
                    held(pool, accT_done, S * 6)
                    held(pool, shift_ld, (ic + 1) * 16)
                    L = shift[:, :, c * H:(c + 1) * H]
                    dT = denT[:, :, :].rearrange("p b h -> p (b h)")
                    pres, t1, t2, Lp = (tiny[:, m, :] for m in range(4))
                    base = (S - 1) * CSTEPS

                    def wide(a):
                        return a.rearrange("p (b h) -> p b h", h=H)
                    seq = [lambda: nc.gpsimd.tensor_scalar(pres, dT, 0.0, 1.0, ALU.is_gt, ALU.mult),
                           lambda: nc.gpsimd.tensor_tensor(wide(t1), L, wide(pres), ALU.mult),
                           lambda: nc.gpsimd.tensor_scalar(t2, pres, ABSENT, -ABSENT, ALU.mult, ALU.add),
                           lambda: nc.gpsimd.tensor_tensor(Lp, t1, t2, ALU.add)]
                    if c == 0:
                        seq += [lambda: nc.gpsimd.tensor_copy(cst[:, :], Lp),
                                lambda: nc.gpsimd.tensor_copy(den[:, :], dT)]
                    else:
                        seq += [lambda: nc.gpsimd.tensor_tensor(t1, Lp, cst[:, :], ALU.subtract),
                                lambda: nc.gpsimd.tensor_scalar(t1, t1, 0.0, 1.0, ALU.is_gt, ALU.mult),
                                lambda: nc.gpsimd.tensor_scalar(t2, t1, -1.0, 1.0, ALU.mult, ALU.add),
                                lambda: nc.gpsimd.tensor_tensor(t1, t1, Lp, ALU.mult),
                                lambda: nc.gpsimd.tensor_tensor(t2, t2, cst[:, :], ALU.mult),
                                lambda: nc.gpsimd.tensor_tensor(t1, t1, t2, ALU.add),
                                lambda: nc.gpsimd.tensor_tensor(abarg[:, 0, :], cst[:, :], t1, ALU.subtract),
                                lambda: nc.gpsimd.tensor_tensor(abarg[:, 1, :], Lp, t1, ALU.subtract),
                                lambda: nc.gpsimd.tensor_copy(cst[:, :], t1)]
                    for m, f in enumerate(seq):
                        f().then_inc(mstep, 1)
                        held(pool, mstep, base + m + 1)
                    m = len(seq)
                    if c > 0:
                        pool.sem_inc(ab_arg, 1)
                        held(pool, ab_done, ic * (n - 1) + c)
                        for f in (lambda: nc.gpsimd.tensor_tensor(den[:, :], den[:, :], ab[:, 0, :], ALU.mult),
                                  lambda: nc.gpsimd.tensor_tensor(t2, dT, ab[:, 1, :], ALU.mult),
                                  lambda: nc.gpsimd.tensor_tensor(den[:, :], den[:, :], t2, ALU.add)):
                            f().then_inc(mstep, 1)
                            m += 1
                            held(pool, mstep, base + m)
                    pool.sem_inc(mstep, CSTEPS - m)
                    if c == n - 1:
                        pool.sem_inc(den_fin, 1)

                def merge(S, c, piece, count):
                    A = accT[:, :, :, :].rearrange("p b (q h) f -> p (b q) h f", q=NQ)[:, bass.ds(piece, 1), :, :]\
                        .rearrange("p a h f -> p (a h) f")
                    Oq = O[:, :, :, :].rearrange("p b (q h) f -> p (b q) h f", q=NQ)[:, bass.ds(piece, 1), :, :]\
                        .rearrange("p a h f -> p (a h) f")

                    def factor(w):
                        return ab[:, w, :].rearrange("p (a h) -> p a h", h=4)[:, bass.ds(piece, 1), :]\
                            .rearrange("p a h -> p (a h)").unsqueeze(2).to_broadcast([P, 4, F])
                    if c == 0:
                        nc.gpsimd.tensor_copy(Oq, A).then_inc(merged, 1)
                        held(pool, merged, count + 1)
                        pool.sem_inc(merged, 2)
                        return
                    tq = tmp[:, 0:4, :]
                    nc.gpsimd.tensor_tensor(tq, A, factor(1), ALU.mult).then_inc(merged, 1)
                    nc.gpsimd.tensor_tensor(Oq, Oq, factor(0), ALU.mult).then_inc(merged, 1)
                    held(pool, merged, count + 2)
                    nc.gpsimd.tensor_tensor(Oq, Oq, tq, ALU.add).then_inc(merged, 1)
                    held(pool, merged, count + 3)

                FST = 6

                def finish(ic, ib, count):
                    rb = rden[:, :].rearrange("p (b h) -> p b h", h=H)[:, bass.ds(ib, 1), :]\
                        .rearrange("p a h -> p (a h)").unsqueeze(2).to_broadcast([P, H, F])
                    Ob = O[:, bass.ds(ib, 1), :, :].rearrange("p a h f -> p (a h) f")
                    rs = res[:, bass.ds(ib, 1), :].rearrange("p a f -> p (a f)")
                    xb = x1c[:, bass.ds(ib, 1), :].rearrange("p a f -> p (a f)")
                    t = tmp
                    seq = [lambda: nc.gpsimd.tensor_tensor(t[:, :, :], Ob, rb, ALU.mult),
                           lambda: nc.gpsimd.tensor_tensor(t[:, 0:4, :], t[:, 0:4, :], t[:, 4:8, :], ALU.add),
                           lambda: nc.gpsimd.tensor_tensor(t[:, 0:2, :], t[:, 0:2, :], t[:, 2:4, :], ALU.add),
                           lambda: nc.gpsimd.tensor_tensor(t[:, 0, :], t[:, 0, :], t[:, 1, :], ALU.add),
                           lambda: nc.gpsimd.tensor_tensor(t[:, 0, :], t[:, 0, :], pb[:, :], ALU.add),
                           lambda: nc.gpsimd.tensor_tensor(rs, t[:, 0, :], xb, ALU.add)]
                    for m, f in enumerate(seq):
                        f().then_inc(fstep, 1)
                        held(pool, fstep, count + m + 1)

                def store(ic):
                    pool.dma_start(out_v[:, bass.ds(ic * IB, IB), :], res[:, :, :]).then_inc(out_st, 16)

                def shifts(ic):
                    pool.dma_start(shift[:, :, :].rearrange("p b k -> p (b k)"), shift_dram[bass.ds(ic * P, P), :])\
                        .then_inc(shift_ld, 16)

                def step(S, half, ic, c, first, par, early):
                    pc = (c - 1) % n
                    pic = ic if c > 0 else ic - 1
                    last_class = pc == n - 1 and not first
                    for q in range(4):
                        for u in range(2):
                            stage(S, c, q, u, first and q == 0)
                        if c == 1 and not early:
                            if q == 0:
                                held(pool, rden_ok, ic)
                                held(pool, x1_ld, ic * 16)
                            finish(ic - 1, q, (ic - 1) * (FST * IB) + q * FST)
                            if q == 3:
                                store(ic - 1)
                    if last_class:
                        pool.dma_start(x1c[:, :, :].rearrange("p b f -> p (b f)"), x1_dram[bass.ds(pic * P, P), :])\
                            .then_inc(x1_ld, 16)
                    if not first:
                        scales(S, pic, pc)
                    if c == 0:
                        shifts(ic)
                    with pool.Fori(4, 12) as q:
                        stage(S, c, q, 0)
                        stage(S, c, q, 1)
                        if not first:
                            merge(S, pc, q - 4, (S - 1) * PER + (q - 4) * 3)
                    with pool.Fori(12, NT // 2) as q:
                        stage(S, c, q, 0)
                        stage(S, c, q, 1)
                    if c == 1 and not early:
                        held(pool, out_st, ic * 16)

                def tail(S, ic):
                    pool.dma_start(x1c[:, :, :].rearrange("p b f -> p (b f)"), x1_dram[ic * P:(ic + 1) * P, :])\
                        .then_inc(x1_ld, 16)
                    scales(S, ic, n - 1)
                    with pool.Fori(0, 2 * IB) as q:
                        merge(S, n - 1, q, (S - 1) * PER + q * 3)
                    pool.wait_ge(rden_ok, NI)
                    pool.wait_ge(x1_ld, NI * 16)
                    with pool.Fori(0, IB) as q:
                        finish(ic, q, ic * (FST * IB) + q * FST)
                    store(ic)
                    pool.wait_ge(out_st, NI * 16)

                class_steps(pool, kvals, step, tail)
            both_paths(pool, "Pool", program)

        @block.scalar
        def _(act):
            link = Chain(act, astep)
            for dst, w, bvec in ((qw, Qw, Qb), (kw, Kw, Kb), (vw, Vw, Vb)):
                act.dma_start(dst[0:F, :], w).then_inc(ld_l1, 16)
                act.dma_start(dst[F:F + 1, :], bvec.unsqueeze(0)).then_inc(ld_l1, 16)
            for k in range(KC):
                act.dma_start(av[:, :, k, :], a1[k].rearrange("(c p) h -> p c h", p=P)).then_inc(ld_l1, 16)
            act.dma_start(pw[:, :, :], Pw.rearrange("(h d) f -> d h f", d=F)).then_inc(ld_l1, 16)
            act.dma_start(pb[:, :], Pb.partition_broadcast(P)).then_inc(ld_l1, 16)
            act.wait_ge(ln_var, 1)
            nc.scalar.activation(stat[:, 4, :], stat[:, 2, :], ACT.Sqrt).then_inc(ln_std, 1)
            act.wait_ge(dshift, 1)
            nc.scalar.activation(th0[:, :], d0[:, :], ACT.Exp, scale=1.0 - SLOPE).then_inc(dexp, 1)
            nc.scalar.activation(W0d[:, :, 0], d0[:, :], ACT.Exp, scale=SLOPE).then_inc(dexp, 1)
            for g in range(NI):
                act.wait_ge(rrow_z, g + 1)
                nc.scalar.activation(r0[:, g * CH:(g + 1) * CH], r0[:, g * CH:(g + 1) * CH], ACT.Exp,
                                     scale=-(1.0 - SLOPE)).then_inc(rrow_done, 1)

            def cast(ic, g):
                if not isinstance(ic, int) or ic * NG + g >= 2:
                    act.wait_ge(tg_done, (ic * NG + g - 1) * IB)
                act.wait_ge(raw_ld[g], (ic + 1) * 16)
                nc.scalar.activation(abf[:, g % 2, :, :], raw[:, g, :, :], ACT.Copy).then_inc(cast_done, 1)

            def positive(ic, g, begin=False):
                if not begin:
                    act.wait_ge(t0_made, (ic - 1) * NT + (g + 1) * G8)
                act.wait_ge(ev_done, (ic * NG + g + 1) * IB)
                if not isinstance(ic, int) or ic * NG + g > 0:
                    act.wait_ge(sq_used, ic * NG + g)
                nc.scalar.activation(sqc[:, :, :], code0[:, g * G8:(g + 1) * G8, :], ACT.Square, bias=halfneg[:, :])\
                    .then_inc(sq_made, 1)
                nc.scalar.activation(pos0[:, g * G8:(g + 1) * G8, :], code0[:, g * G8:(g + 1) * G8, :], ACT.Relu)\
                    .then_inc(pos_done, 1)

            act.wait_ge(consts, 7 + CL)
            cast(0, 0)
            cast(0, 1)
            for g in range(2, NG):
                cast(0, g)
                positive(0, g - 2, True)

            def chunk(ic, second):
                for g in range(NG):
                    cast(ic, g)
                    if g < 2:
                        positive(ic - 1, NG - 2 + g, second)
                    else:
                        positive(ic, g - 2)
            chunk(1, True)
            with act.Fori(2, NI) as ic:
                chunk(ic, False)
            positive(NI - 1, NG - 2)
            positive(NI - 1, NG - 1)
            act.wait_ge(elu_in, 1)
            nc.scalar.activation(sq1[:, :, :], sq1[:, :, :], ACT.Exp).then_inc(elu_exp, 1)
            act.wait_ge(ln_var, 2)
            nc.scalar.activation(stat[:, 4, :], stat[:, 2, :], ACT.Sqrt).then_inc(ln_std, 1)
            for g in range(NI):
                act.wait_ge(aT_z, g + 1)
                nc.scalar.activation(rT[:, g * CH:(g + 1) * CH], rT[:, g * CH:(g + 1) * CH], ACT.Exp,
                                     scale=-(1.0 - SLOPE)).then_inc(rT_done, 1)
            act.wait_ge(tab_in, 1)
            nc.scalar.activation(th[:, :, :], bt[:, :, :], ACT.Exp, scale=1.0 - SLOPE).then_inc(tab_exp, 1)
            nc.scalar.activation(dd[:, :, :], bt[:, :, :], ACT.Exp, scale=SLOPE).then_inc(tab_exp, 1)
            act.wait_ge(x1_st, 16)
            for t in range(NT):
                act.wait_ge(vp_ps, t + 1)
                nc.scalar.activation(vp[:, t, :], ps[:, 4 + t % 4, :], ACT.Copy).then_inc(vp_sb, 1)
            act.wait_ge(vp_sb, NT)
            act.wait_ge(tab_exp, 2)
            act.sem_inc(pre_end, 1)
            act.wait_ge(pre_end, 5)

            def program(kvals):
                n = len(kvals)

                def mask(S, c, q, u, early=False):
                    jt = q * 2 + u
                    num = S * NT + jt
                    if not early:
                        act.wait_ge(mask_made, num - 1)
                        held(act, t_made, (num - 1) * NQ)
                    nc.scalar.activation(Mt[:, u, :], code[:, bass.ds(jt, 1), :].rearrange("p a i -> p (a i)"),
                                         ACT.Abs, bias=classneg[:, c:c + 1]).then_inc(abs_done, 1)
                    act.wait_ge(abs_done, num + 1)
                    nc.scalar.activation(M[:, u, :], Mt[:, u, :], ACT.Relu, bias=onesF[:, 0:1], scale=-1.0)\
                        .then_inc(mask_made, 1)

                def factors(ic, c):
                    act.wait_ge(ab_arg, ic * (n - 1) + c)
                    nc.scalar.activation(ab[:, :, :], abarg[:, :, :], ACT.Exp).then_inc(ab_done, 1)

                def transposed_sums(S, b):
                    act.wait_ge(acc_tr, S * 6 + b + 1)
                    tr = ps[:, 6 + b % 2, :].rearrange("p (b c) -> p b c", b=IB)
                    if b % 3 < 2:
                        pair = (b // 3) * 2 + b % 3
                        dst, src = accT[:, :, 2 * pair:2 * pair + 2, :], tr.rearrange("p b (h f) -> p b h f", f=F)
                    else:
                        Q = b // 3
                        dst, src = denT[:, :, Q * 4:Q * 4 + 4], tr.rearrange("p b (h r) -> p b h r", r=32)[:, :, :, 0]
                    nc.scalar.activation(dst, src, ACT.Copy).then_inc(accT_done, 1)

                def evacuate(S, begin=False):
                    act.wait_ge(pe_quad, (S + 1) * (NT * NQ))
                    for b in range(6):
                        if not begin:
                            act.wait_ge(acc_tr, (S - 1) * 6 + b + 1)
                        nc.scalar.activation(accS[:, b, :], ps[:, b, :], ACT.Copy).then_inc(acc_ev, 1)

                def step(S, half, ic, c, first, par, early):
                    if c == 0:
                        held(act, code_ld[0], (ic + 1) * 16)
                    pc = (c - 1) % n
                    for q in range(4):
                        mask(S, c, q, 0, first and q == 0)
                        mask(S, c, q, 1, first and q == 0)
                        if q == 0 and not first:
                            evacuate(S - 1, early)
                        if not first and q > 0:
                            if q == 1 and not early:
                                act.wait_ge(merged, (S - 1) * (3 * 2 * IB))
                            transposed_sums(S - 1, 2 * q - 2)
                            transposed_sums(S - 1, 2 * q - 1)
                    if not first and pc > 0:
                        factors(ic if c > 0 else ic - 1, pc)
                    with act.Fori(2, NT // 8) as q2:
                        for e in range(2):
                            mask(S, c, q2 * 2 + e, 0)
                            mask(S, c, q2 * 2 + e, 1)
                    if c == 0:
                        held(act, code_ld[1], (ic + 1) * 16)
                    with act.Fori(NT // 8, NT // 4) as q2:
                        for e in range(2):
                            mask(S, c, q2 * 2 + e, 0)
                            mask(S, c, q2 * 2 + e, 1)

                def tail(S, ic):
                    evacuate(S - 1)
                    act.wait_ge(merged, (S - 1) * (3 * 2 * IB))
                    for b in range(6):
                        transposed_sums(S - 1, b)
                    factors(ic, n - 1)

                class_steps(act, kvals, step, tail)
            both_paths(act, "Activation", program)

        @block.vector
        def _(dve):
            link = Chain(dve, vstep)
            dve.wait_ge(ld_x, 16)
            layernorm(dve, link, xs[:, :, :], h0[:, :, :], sq0, 1)
            dve.wait_ge(w0T_ps, 1)
            nc.vector.tensor_copy(w0T[:, :], ps[0:F, 4, 0:F]).then_inc(w0T_sb, 1)
            dve.wait_ge(wa_ps, 1)
            nc.vector.tensor_copy(w0s[:, F:F + 2], ps[0:F, 5, 0:2]).then_inc(wa_sb, 1)
            nc.vector.tensor_copy(wrep[:, :], ps[0:F, 5, 0:1].to_broadcast([F, P])).then_inc(wa_sb, 1)
            for g in range(NI):
                dve.wait_ge(hT_ps, g + 1)
                nc.vector.tensor_copy(h0T[:, g * CH:(g + 1) * CH], ps[0:F, g % 4, :]).then_inc(hT_sb, 1)
            for g in range(NI):
                dve.wait_ge(wh_ps, g + 1)
                nc.vector.tensor_copy(wh[:, g * IB:(g + 1) * IB, :],
                                      ps[:, 4 + g % 4, 0:IB * (F + 2)].rearrange("p (t f) -> p t f", f=F + 2))\
                    .then_inc(wh_sb, 1)
            dve.wait_ge(wh_sb, NI)
            nc.vector.tensor_reduce(dm[:, 0:1], wh[:, :, F + 1], AX.X, ALU.max).then_inc(dmax_in, 1)
            nc.vector.tensor_reduce(whsum[:, :], wh[:, :, 0:F].rearrange("p t f -> p f t"), AX.X, ALU.add)\
                .then_inc(mean_in, 1)
            dve.wait_ge(dmax_out, 1)
            nc.vector.tensor_scalar(d0[:, :], wh[:, :, F + 1], dm[:, 1:2], None, ALU.subtract).then_inc(dshift, 1)
            for g in range(NI):
                dve.wait_ge(rrow_ps, g + 1)
                nc.vector.tensor_scalar(r0[:, g * CH:(g + 1) * CH], ps[:, g % 4, :], dm[:, 1:2], 0.0, ALU.add,
                                        ALU.max).then_inc(rrow_z, 1)
            dve.wait_ge(dexp, 2)
            nc.vector.tensor_tensor(W0e[:, :, :], wh[:, :, 0:F], W0d[:, :, 0:1].to_broadcast([P, NT, F]),
                                    ALU.mult).then_inc(w0_ready, 1)
            nc.vector.tensor_copy(W0d[:, :, 1:32], W0d[:, :, 0:1].to_broadcast([P, NT, 31])).then_inc(w0_ready, 1)
            nc.vector.tensor_tensor(pairI[:, :], identF[:, 0:F], identF[:, F:2 * F], ALU.add).then_inc(w0_ready, 1)
            nc.vector.tensor_reduce(sel[:, :], identF[:, :].rearrange("p (a b) -> p a b", b=32)[:, :, 0], AX.X, ALU.add)\
                .then_inc(w0_ready, 1)
            dve.wait_ge(mean_ps, 1)
            nc.vector.tensor_copy(whmean[:, :], ps[:, 7, 0:F]).then_inc(mean_sb, 1)
            dve.wait_ge(rrow_done, NI)
            dve.wait_ge(mean_sb, 1)
            vbase = link.n
            FIN = 9

            def evacuate(ic, g, b):
                dve.wait_ge(tg_done, (ic * NG + g) * IB + b + 1)
                src = ps[:, b, :].bitcast(bf16).rearrange("p (t i) -> p t i", i=P)
                nc.vector.tensor_scalar(code0[:, g * G8:(g + 1) * G8, b * P:(b + 1) * P], src, float(KC - 1),
                                        -1.0, ALU.min, ALU.max).then_inc(ev_done, 1)

            def probs(ic, jt, begin):
                if not begin or jt >= TS:
                    dve.wait_ge(t0_used, ic * NT + jt - TS + 1)
                nc.vector.scalar_tensor_tensor(out=T0[:, jt % TS, :], in0=r0[:, bass.ds(ic * CH, CH)],
                                               scalar=th0[:, jt:jt + 1], in1=pos0[:, jt, :], op0=ALU.max,
                                               op1=ALU.min).then_inc(t0_made, 1)

            def sums_out(ic):
                dve.wait_ge(t0_used, (ic + 1) * NT)
                nc.vector.tensor_copy(A0s[:, 0, :], ps[:, 5, :]).then_inc(a0_sb, 1)
                nc.vector.tensor_copy(A0s[:, 1, :], ps[:, 7, :]).then_inc(a0_sb, 1)

            def finish(ic):
                dve.wait_ge(a0_tr, ic + 1)
                at = ps[:, 6, 0:IB * (F + 1)].rearrange("p (b f) -> p b f", f=F + 1)
                dn, pres, absent, rec = (den0[:, m, :] for m in range(4))

                def wide(a):
                    return a.unsqueeze(2).to_broadcast([P, IB, F])
                hv = h0[:, bass.ds(ic * IB, IB), :]
                mean_b = whmean[:, :].unsqueeze(1).to_broadcast([P, IB, F])
                seq = [lambda: nc.vector.tensor_copy(dn, at[:, :, F]),
                       lambda: nc.vector.tensor_scalar(pres, dn, 0.0, None, ALU.is_gt),
                       lambda: nc.vector.tensor_scalar(absent, pres, -1.0, 1.0, ALU.mult, ALU.add),
                       lambda: nc.vector.tensor_tensor(dn, dn, absent, ALU.add),
                       lambda: nc.vector.reciprocal(rec, dn),
                       lambda: nc.vector.tensor_tensor(rec, rec, pres, ALU.mult),
                       lambda: nc.vector.tensor_tensor(fin0[:, 0, :, :], at[:, :, 0:F], wide(rec), ALU.mult),
                       lambda: nc.vector.tensor_tensor(fin0[:, 1, :, :], mean_b, wide(absent), ALU.mult),
                       lambda: nc.vector.tensor_tensor(hv, fin0[:, 0, :, :], fin0[:, 1, :, :], ALU.add)]
                assert len(seq) == FIN
                for m, f in enumerate(seq):
                    f().then_inc(a0_fin, 1)
                    dve.wait_ge(a0_fin, ic * FIN + m + 1)

            for g in range(NG):
                for b in range(IB):
                    evacuate(0, g, b)

            def chunk(ic, second, edges=True):
                for g in range(NG):
                    dve.wait_ge(sq_made, (ic - 1) * NG + g + 1)
                    dve.wait_ge(pos_done, (ic - 1) * NG + g + 1)
                    if edges:
                        dve.wait_ge(code_st[g], ic * 16)
                    for b in range(IB):
                        if edges:
                            evacuate(ic, g, b)
                        if g == 0 and b == 2 and not second:
                            sums_out(ic - 2)
                        for e in range(G8 // IB):
                            probs(ic - 1, g * G8 + b * (G8 // IB) + e, second)
                        if g == 1 and b == 1 and not second:
                            finish(ic - 2)
            chunk(1, True)
            with dve.Fori(2, NI) as ic:
                chunk(ic, False)
            chunk(NI, False, edges=False)
            sums_out(NI - 1)
            finish(NI - 1)
            for g in range(NG):
                dve.wait_ge(code_st[g], NI * 16)
            dve.wait_ge(flag_ps, 1)
            link(nc.vector.tensor_reduce(flagcol[:, 0:1], ps[0:1, 4, :], AX.X, ALU.max))
            nc.vector.tensor_scalar(flagcol[:, 1:2], flagcol[:, 0:1], 0.25 * N * N / CH, None, ALU.is_gt)\
                .then_inc(flag_sum, 1)
            dve.wait_ge(flag_sum, 1)
            nc.vector.tensor_copy(flagi[0:1, :], flagcol[:, 1:2]).then_inc(flag_done, 1)
            nc.vector.tensor_scalar(sq1[:, :, :], h0[:, :, :], 0.0, None, ALU.min).then_inc(elu_in, 1)
            link(nc.vector.scalar_tensor_tensor(out=xs[:, :, :], in0=h0[:, :, :], scalar=0.0, in1=xs[:, :, :],
                                                op0=ALU.max, op1=ALU.add))
            dve.wait_ge(elu_exp, 1)
            link(nc.vector.scalar_tensor_tensor(out=xs[:, :, :], in0=sq1[:, :, :], scalar=-1.0, in1=xs[:, :, :],
                                                op0=ALU.add, op1=ALU.add))
            layernorm(dve, link, xs[:, :, :], h1[:, :, :], sq1[:, :, :], 2)
            link(nc.vector.memset(hT[F:F + 1, :], 1.0))
            link(nc.vector.memset(sa[:, KHV:KH], 0.0))
            link(nc.vector.memset(sbm[:, KHV:KH], 0.0))
            dve.wait_ge(wT_ps, 3)
            for dst, bank in ((qT, 4), (kT, 5)):
                nc.vector.tensor_copy(dst[:, :, :], ps[:, bank, 0:DC * (F + 1)].rearrange("p (c f) -> p c f", f=F + 1))\
                    .then_inc(wT_sb, 1)
            for hh in range(2):
                nc.vector.tensor_copy(vT[:, 4 * hh:4 * hh + 4, :],
                                      ps[0:F, 6 + hh, 0:4 * (F + 1)].rearrange("p (h f) -> p h f", f=F + 1))\
                    .then_inc(wT_sb, 1)
            for g in range(NI):
                dve.wait_ge(hT_ps, NI + g + 1)
                nc.vector.tensor_copy(hT[0:F, g * CH:(g + 1) * CH], ps[0:F, g % 4, :]).then_inc(hT_sb, 1)
            dve.wait_ge(s_ps, 1)
            nc.vector.tensor_copy(sa[:, 0:KHV], ps[0:F + 1, 4, 0:KHV]).then_inc(s_sb, 1)
            nc.vector.tensor_copy(sbm[:, 0:KHV], ps[0:F + 1, 5, 0:KHV]).then_inc(s_sb, 1)
            nc.vector.tensor_copy(vpw[:, :], ps[0:F + 1, 6, :]).then_inc(s_sb, 1)
            for g in range(NI):
                dve.wait_ge(bT_ps, g + 1)
                nc.vector.tensor_reduce(bm8[:, g:g + 1], ps[0:KH, g % 4, :], AX.X, ALU.max).then_inc(bT_red, 1)
            dve.wait_ge(bT_red, NI)
            link(nc.vector.tensor_reduce(bm8[:, NI:NI + 1], bm8[:, 0:NI], AX.X, ALU.max))
            nc.vector.tensor_copy(bmrep[:, :], bm8[:, NI:NI + 1].to_broadcast([KH, P])).then_inc(bmx_in, 1)
            dve.wait_ge(bmx_ps, 1)
            link(nc.vector.tensor_copy(bmx[:, :], ps[:, 7, 0:KH]))
            for g in range(NI):
                dve.wait_ge(aT_ps, g + 1)
                nc.vector.tensor_scalar(rT[:, g * CH:(g + 1) * CH], ps[0:KH, g % 4, :], bm8[:, NI:NI + 1], 0.0,
                                        ALU.add, ALU.max).then_inc(aT_z, 1)
            for g in range(2 * NI):
                dve.wait_ge(ab_ps, g + 1)
                t0 = (g % NI) * IB
                dst = (bt if g < NI else LL)[:, t0:t0 + IB, :]
                nc.vector.tensor_tensor(dst, ps[:, 4 + g % 3, 0:IB * KH].rearrange("p (t c) -> p t c", c=KH),
                                        bmx[:, :].unsqueeze(1).to_broadcast([P, IB, KH]),
                                        ALU.subtract if g < NI else ALU.add).then_inc(ab_sb, 1)
            dve.wait_ge(ab_sb, 2 * NI)
            nc.vector.tensor_scalar(bt[:, :, :], bt[:, :, :], 0.0, None, ALU.min).then_inc(tab_in, 1)
            nc.vector.scalar_tensor_tensor(out=LL[:, :, :], in0=LL[:, :, :], scalar=SLOPE, in1=LL[:, :, :],
                                           op0=ALU.mult, op1=ALU.max).then_inc(shift_ok, 1)
            dve.wait_ge(shift_ok, 1)
            dve.wait_ge(tab_in, 1)
            dve.sem_inc(pre_end, 1)
            dve.wait_ge(pre_end, 5)

            def program(kvals):
                n = len(kvals)

                def probs(S, c, par, q, u, early=False):
                    jt = q * 2 + u
                    num = S * NT + jt
                    dve.wait_ge(mask_made, num + 1)
                    for h in range(H):
                        if h % 4 == 0 and not early:
                            dve.wait_ge(pe_quad, (num - 2) * NQ + h // 4 + 1)
                        last = nc.vector.scalar_tensor_tensor(
                            out=T[:, u, h, :], in0=R[:, par, h, :],
                            scalar=th[:, bass.ds(jt, 1), c * H + h:c * H + h + 1].rearrange("p a b -> p (a b)"),
                            in1=M[:, u, :], op0=ALU.max, op1=ALU.mult)
                        if h % 4 == 3:
                            last.then_inc(t_made, 1)

                def recip(S, ic):
                    dve.wait_ge(den_fin, ic + 1)
                    nc.vector.reciprocal(rden[:, :], den[:, :]).then_inc(rden_ok, 1)

                def step(S, half, ic, c, first, par, early):
                    dve.wait_ge(r_ld[par], (half + 1) * 16)
                    probs(S, c, par, 0, 0, first)
                    probs(S, c, par, 0, 1, first)
                    probs(S, c, par, 1, 0)
                    probs(S, c, par, 1, 1)
                    with dve.Fori(1, NT // 4) as q2:
                        for e in range(2):
                            probs(S, c, par, q2 * 2 + e, 0)
                            probs(S, c, par, q2 * 2 + e, 1)
                    if c == 0 and not first:
                        recip(S, ic - 1)

                class_steps(dve, kvals, step, lambda S, ic: recip(S, ic))
            both_paths(dve, "DVE", program)

        @block.tensor
        def _(pe):
            pe.wait_ge(consts, 7 + CL)
            pe.wait_ge(ld_w0, 48)
            nc.tensor.transpose(ps[0:F, 4, 0:F], w0s[:, 0:F], identF[0:F, 0:F]).then_inc(w0T_ps, 1)
            pe.wait_ge(w0T_sb, 1)
            nc.tensor.matmul(ps[0:F, 5, 0:2], w0T[:, :], a0s[:, :], start=True, stop=True).then_inc(wa_ps, 1)

            def transposed(src, done, base):
                for g in range(NI):
                    if base + g >= 4:
                        pe.wait_ge(hT_sb, base + g - 3)
                    for b in range(IB):
                        last = nc.tensor.transpose(ps[0:F, g % 4, b * P:(b + 1) * P], src[:, g * IB + b, :],
                                                   identF[:, :])
                    last.then_inc(hT_ps, 1)
            pe.wait_ge(ln_done, 1)
            transposed(h0, ln_done, 0)
            pe.wait_ge(wa_sb, 2)
            for g in range(NI):
                pe.wait_ge(hT_sb, g + 1)
                if g >= 4:
                    pe.wait_ge(wh_sb, g - 3)
                for b in range(IB):
                    t = g * IB + b
                    last = nc.tensor.matmul(ps[:, 4 + g % 4, b * (F + 2):(b + 1) * (F + 2)],
                                            h0T[:, t * P:(t + 1) * P], w0s[:, :], start=True, stop=True)
                last.then_inc(wh_ps, 1)
            for g in range(NI):
                if g >= 4:
                    pe.wait_ge(rrow_z, g - 3)
                nc.tensor.matmul(ps[:, g % 4, :], wrep[:, :], h0T[:, g * CH:(g + 1) * CH], start=True, stop=True)\
                    .then_inc(rrow_ps, 1)
            pe.wait_ge(mean_in, 1)
            pe.wait_ge(wh_sb, NI)
            nc.tensor.matmul(ps[:, 7, 0:F], meanmat[:, :], whsum[:, :], start=True, stop=True).then_inc(mean_ps, 1)
            pe.wait_ge(w0_ready, 4)
            pe.wait_ge(mean_sb, 1)
            pe.wait_ge(rrow_z, NI)
            nc.tensor.matmul(ps[0:1, 4, :], zerosB[:, 0:1], zerosB[:, :], start=True, stop=False,
                             skip_group_check=True)

            def edges_T(ic, g, b):
                if b == 0:
                    pe.wait_ge(cast_done, ic * NG + g + 1)
                if not isinstance(ic, int) or ic * NG + g > 0:
                    pe.wait_ge(ev_done, (ic * NG + g - 1) * IB + b + 1)
                for e in range(G8):
                    blk = abf[:, g % 2, b, e * P:(e + 1) * P]
                    last = nc.tensor.transpose(ps[:, b, :].bitcast(bf16)[:, e * P:(e + 1) * P], blk, identB[:, :])
                last.then_inc(tg_done, 1)

            def squares(ic, g):
                pe.wait_ge(sq_made, ic * NG + g + 1)
                for e in range(G8):
                    last = nc.tensor.matmul(ps[0:1, 4, :], onesB[:, :], sqc[:, e, :], start=False, stop=False,
                                            skip_group_check=True)
                last.then_inc(sq_used, 1)

            def products0(ic, jq, begin):
                pe.wait_ge(t0_made, ic * NT + jq * 4 + 4)
                if jq == 0 and not begin:
                    pe.wait_ge(a0_sb, ic * 2)
                for e in range(4):
                    jt = jq * 4 + e
                    p0 = F * (e % 2)
                    nc.tensor.matmul(ps[p0:p0 + F, 5, :], W0e[:, jt, :], T0[:, jt % TS, :], start=(jt < 2),
                                     stop=(jt >= NT - 2))
                for e in range(4):
                    jt = jq * 4 + e
                    nc.tensor.matmul(ps[32 * e:32 * e + 32, 7, :], W0d[:, jt, :], T0[:, jt % TS, :], start=(jt < 4),
                                     stop=(jt >= NT - 4), tile_position=(0, 32 * e)).then_inc(t0_used, 1)

            def sums_T(ic):
                pe.wait_ge(a0_sb, (ic + 1) * 2)
                for b in range(IB):
                    o = b * (F + 1)
                    nc.tensor.matmul(ps[:, 6, o:o + F], A0s[:, 0, b * P:(b + 1) * P], pairI[:, :], start=True,
                                     stop=True)
                    last = nc.tensor.matmul(ps[:, 6, o + F:o + F + 1], A0s[:, 1, b * P:(b + 1) * P], sel[:, :],
                                            start=True, stop=True)
                last.then_inc(a0_tr, 1)

            for g in range(NG):
                for b in range(IB):
                    edges_T(0, g, b)
                if g > 0:
                    squares(0, g - 1)

            def chunk(ic, second, edges=True):
                for g in range(NG):
                    for b in range(IB):
                        if edges:
                            edges_T(ic, g, b)
                        u = g * IB + b
                        if u == 1 and not second:
                            products0(ic - 2, NT // 4 - 1, False)
                        if u == 4 and not second:
                            sums_T(ic - 2)
                        if u % 2 == 1 and u > 1:
                            products0(ic - 1, (u - 3) // 2, second)
                    if g == 0:
                        squares(ic - 1, NG - 1)
                    elif edges:
                        squares(ic, g - 1)
            chunk(1, True)
            with pe.Fori(2, NI) as ic:
                chunk(ic, False)
            chunk(NI, False, edges=False)
            products0(NI - 1, NT // 4 - 1, False)
            sums_T(NI - 1)
            nc.tensor.matmul(ps[0:1, 4, :], zerosB[:, 0:1], zerosB[:, :], start=False, stop=True,
                             skip_group_check=True).then_inc(flag_ps, 1)
            pe.wait_ge(ld_l1, 16 * (6 + KC + 2))
            pe.wait_ge(flag_sum, 1)
            pe.wait_ge(a0_fin, NI * 9)
            for w, bank in ((qw, 4), (kw, 5)):
                for c in range(DC):
                    last = nc.tensor.transpose(ps[:, bank, c * (F + 1):(c + 1) * (F + 1)], w[:, c * P:(c + 1) * P],
                                               identF[0:F + 1, 0:F + 1])
                last.then_inc(wT_ps, 1)
            for h in range(H):
                last = nc.tensor.transpose(ps[0:F, 6 + h // 4, (h % 4) * (F + 1):(h % 4 + 1) * (F + 1)],
                                           vw[:, h * F:(h + 1) * F], identF[0:F + 1, 0:F + 1])
            last.then_inc(wT_ps, 1)
            pe.wait_ge(wT_sb, 4)
            for w, bank, half in ((qT, 4, 0), (kT, 5, 1)):
                for c in range(DC):
                    nc.tensor.matmul(ps[0:F + 1, bank, 0:KHV], w[:, c, :],
                                     av[:, half * DC + c, :, :].rearrange("p k h -> p (k h)"), start=(c == 0),
                                     stop=(c == DC - 1))
            for h in range(H):
                last = nc.tensor.matmul(ps[0:F + 1, 6, h * F:(h + 1) * F], vT[:, h, :], pw[:, h, :], start=True,
                                        stop=True)
            last.then_inc(s_ps, 1)
            pe.wait_ge(ln_done, 2)
            transposed(h1, ln_done, NI)
            pe.wait_ge(hT_sb, 2 * NI)
            pe.wait_ge(s_sb, 3)
            for g in range(NI):
                if g >= 4:
                    pe.wait_ge(bT_red, g - 3)
                nc.tensor.matmul(ps[0:KH, g % 4, :], sbm[:, :], hT[:, g * CH:(g + 1) * CH], start=True, stop=True)\
                    .then_inc(bT_ps, 1)
            pe.wait_ge(bmx_in, 1)
            nc.tensor.matmul(ps[:, 7, 0:KH], bmrep[:, :], identF[0:KH, 0:KH], start=True, stop=True).then_inc(bmx_ps, 1)
            for g in range(NI):
                if g >= 4:
                    pe.wait_ge(aT_z, g - 3)
                nc.tensor.matmul(ps[0:KH, g % 4, :], sa[:, :], hT[:, g * CH:(g + 1) * CH], start=True, stop=True)\
                    .then_inc(aT_ps, 1)
            for g in range(2 * NI):
                if g >= 3:
                    pe.wait_ge(ab_sb, g - 2)
                for b in range(IB):
                    t = (g % NI) * IB + b
                    last = nc.tensor.matmul(ps[:, 4 + g % 3, b * KH:(b + 1) * KH], hT[:, t * P:(t + 1) * P],
                                            (sbm if g < NI else sa)[:, :], start=True, stop=True)
                last.then_inc(ab_ps, 1)
            pe.wait_ge(ab_sb, 2 * NI)
            for t in range(NT):
                if t >= 4:
                    pe.wait_ge(vp_sb, t - 3)
                nc.tensor.matmul(ps[:, 4 + t % 4, :], hT[:, t * P:(t + 1) * P], vpw[:, :], start=True, stop=True)\
                    .then_inc(vp_ps, 1)
            pe.wait_ge(vp_sb, NT)
            pe.wait_ge(aT_z, NI)
            pe.wait_ge(rT_st, 16)
            pe.sem_inc(pre_end, 2)
            pe.wait_ge(pre_end, 5)

            def program(kvals):
                n = len(kvals)

                def products(S, q, u, begin, end, first=False):
                    jt = q * 2 + u
                    num = S * NT + jt
                    pe.wait_ge(w_staged, (num + 1) * 2)
                    for Q in range(NQ):
                        pe.wait_ge(t_made, num * NQ + Q + 1)
                        if begin and not first:
                            pe.wait_ge(acc_ev, (S - 1) * 6 + 3 * Q + 3)
                        for hh in range(4):
                            h = 4 * Q + hh
                            p0 = F * (hh % 2)
                            nc.tensor.matmul(ps[p0:p0 + F, 3 * Q + hh // 2, :], Ws[:, u, h, :], T[:, u, h, :],
                                             start=begin, stop=end)
                        for hh in range(4):
                            h = 4 * Q + hh
                            last = nc.tensor.matmul(ps[32 * hh:32 * hh + 32, 3 * Q + 2, :], Ds[:, u, h, :], T[:, u, h, :],
                                                    start=begin, stop=end, tile_position=(0, 32 * hh))
                        last.then_inc(pe_quad, 1)

                def transposed_sums(S, b, skip=False):
                    pe.wait_ge(acc_ev, S * 6 + b + 1)
                    if not skip:
                        pe.wait_ge(accT_done, S * 6 + b - 1)
                    for i in range(IB):
                        last = nc.tensor.transpose(ps[:, 6 + b % 2, i * P:(i + 1) * P],
                                                   accS[:, b, i * P:(i + 1) * P], identF[:, :])
                    last.then_inc(acc_tr, 1)

                def step(S, half, ic, c, first, par, early):
                    for q in range(3):
                        products(S, q, 0, q == 0, False, first)
                        products(S, q, 1, False, False)
                        if not first:
                            for b in (2 * q, 2 * q + 1):
                                transposed_sums(S - 1, b, early and b < 2)
                    products(S, 3, 0, False, False)
                    products(S, 3, 1, False, False)
                    with pe.Fori(2, NT // 4 - 1) as q2:
                        for e in range(2):
                            products(S, q2 * 2 + e, 0, False, False)
                            products(S, q2 * 2 + e, 1, False, False)
                    products(S, NT // 2 - 2, 0, False, False)
                    products(S, NT // 2 - 2, 1, False, False)
                    products(S, NT // 2 - 1, 0, False, False)
                    products(S, NT // 2 - 1, 1, False, True)

                def tail(S, ic):
                    for b in range(6):
                        transposed_sums(S - 1, b)

                class_steps(pe, kvals, step, tail)
            both_paths(pe, "PE", program)


_INS = ['x', 'adj', 'L0_gnn_W', 'L0_gnn_a', 'L1_gnn_Qw', 'L1_gnn_Qb', 'L1_gnn_Kw', 'L1_gnn_Kb', 'L1_gnn_Vw',
        'L1_gnn_Vb', 'L1_gnn_a', 'L1_gnn_Pw', 'L1_gnn_Pb']


def kernel(**inputs):
    import numpy as _np
    import concourse.bacc as _bacc
    from concourse import mybir as _mybir
    from concourse.bass_utils import run_bass_kernel_spmd as _run

    nc = _bacc.Bacc("TRN2", target_bir_lowering=False, num_devices=1)
    arrays, args = {}, []
    for name in _INS:
        a = _np.ascontiguousarray(inputs[name])
        arrays[f"in_{name}"] = a
        args.append(nc.dram_tensor(f"in_{name}", a.shape, _mybir.dt.from_np(a.dtype), kind="ExternalInput").ap())
    shape = arrays["in_x"].shape
    out = nc.dram_tensor("out_0", shape, _mybir.dt.float32, kind="ExternalOutput").ap()
    two_layer_graph_attention(nc, *args, out)
    r = _run(nc, [arrays], core_ids=[0])
    return r.results[0]["out_0"]
```
